# Optimizing a Trainium2 kernel written in Bass

```python
import numpy as np
import jax
import jax.numpy as jnp

def _softmax(x, axis=-1):
    return jax.nn.softmax(x, axis=axis)
def _gelu(x):
    return jax.nn.gelu(x, approximate=True)
def _silu(x):
    return jax.nn.silu(x)
def _sigmoid(x):
    return jax.nn.sigmoid(x)
def _layernorm(x, axis=-1, eps=1e-5):
    m = jnp.mean(x, axis=axis, keepdims=True)
    v = jnp.var(x, axis=axis, keepdims=True)
    return (x - m) / jnp.sqrt(v + eps)
def _scatter_add(tgt, idx, src, axis=0):
    return tgt.at[idx].add(src)
def _segment_sum(src, seg, n):
    return jax.ops.segment_sum(src, seg, n)

kernel_name = 'mk_conv_seq_d1_conv_nchw256_4309cf'

def setup_inputs(seed: int = 0):
    np.random.seed(seed)
    _w = jnp.asarray
    def _rec_inputs():
        import jax
        import jax.numpy as jnp
        _gk = jax.random.key(seed)
        x = -0.0002091 + 1 * jax.random.normal(jax.random.fold_in(_gk, 1), (32, 256, 56, 56), jnp.float32)
        return x
    x = _rec_inputs()
    def _L0_conv_setup():
        import jax, jax.numpy as jnp
        import numpy as np
        EPS_STD = 1e-06
        EPS_L2 = 1e-12

        def std_weight(w, gain):
            scale = 1.0 / np.sqrt(w.shape[1])
            mean = jnp.mean(w, axis=1, keepdims=True)
            var = jnp.var(w, axis=1, keepdims=True)
            return (w - mean) / jnp.sqrt(var + EPS_STD) * (gain[:, None] * scale)

        def l2_normalize(t):
            n = jnp.linalg.norm(t, axis=-1, keepdims=True)
            return t / jnp.maximum(n, EPS_L2)
        key = jax.random.key(seed)
        ks = jax.random.split(key, 3)
        B, C, H, W = (32, 256, 56, 56)
        num_heads = 8
        return {'x': jax.random.normal(ks[0], (B, C, H, W), dtype=jnp.float32), 'qkv_w': jax.random.normal(ks[1], (3 * C, C), dtype=jnp.float32), 'qkv_b': jnp.zeros((3 * C,), dtype=jnp.float32), 'qkv_gain': jnp.ones((3 * C,), dtype=jnp.float32), 'proj_w': jax.random.normal(ks[2], (C, C), dtype=jnp.float32), 'proj_b': jnp.zeros((C,), dtype=jnp.float32), 'proj_gain': jnp.ones((C,), dtype=jnp.float32), 'temperature': jnp.ones((num_heads, 1, 1), dtype=jnp.float32)}
    _L0_conv_all = _L0_conv_setup()
    _L0_conv_in = {k: v for k, v in _L0_conv_all.items() if k in ('qkv_w', 'qkv_b', 'qkv_gain', 'proj_w', 'proj_b', 'proj_gain', 'temperature', )}
    del _L0_conv_all

    return {
        "x": x,
        "L0_conv_qkv_w": _L0_conv_in["qkv_w"],
        "L0_conv_qkv_b": _L0_conv_in["qkv_b"],
        "L0_conv_qkv_gain": _L0_conv_in["qkv_gain"],
        "L0_conv_proj_w": _L0_conv_in["proj_w"],
        "L0_conv_proj_b": _L0_conv_in["proj_b"],
        "L0_conv_proj_gain": _L0_conv_in["proj_gain"],
        "L0_conv_temperature": _L0_conv_in["temperature"],
    }

def reference(x, L0_conv_qkv_w, L0_conv_qkv_b, L0_conv_qkv_gain, L0_conv_proj_w, L0_conv_proj_b, L0_conv_proj_gain, L0_conv_temperature):
    import jax
    import jax.numpy as jnp
    def _L0_conv_ref(x, qkv_w, qkv_b, qkv_gain, proj_w, proj_b, proj_gain, temperature):
        import jax, jax.numpy as jnp
        import numpy as np
        EPS_STD = 1e-06
        EPS_L2 = 1e-12

        def std_weight(w, gain):
            scale = 1.0 / np.sqrt(w.shape[1])
            mean = jnp.mean(w, axis=1, keepdims=True)
            var = jnp.var(w, axis=1, keepdims=True)
            return (w - mean) / jnp.sqrt(var + EPS_STD) * (gain[:, None] * scale)

        def l2_normalize(t):
            n = jnp.linalg.norm(t, axis=-1, keepdims=True)
            return t / jnp.maximum(n, EPS_L2)
        B, C, H, W = x.shape
        nh = temperature.shape[0]
        dh = C // nh
        N = H * W
        xf = x.reshape(B, C, N)
        wq = std_weight(qkv_w, qkv_gain)
        qkv = jnp.einsum('oc,bcn->bon', wq, xf) + qkv_b[None, :, None]
        qkv = qkv.reshape(B, 3, nh, dh, N)
        q, k, v = (qkv[:, 0], qkv[:, 1], qkv[:, 2])
        q = l2_normalize(q)
        k = l2_normalize(k)
        attn = jnp.einsum('bhdn,bhen->bhde', q, k) * temperature
        attn = jax.nn.softmax(attn, axis=-1)
        out = jnp.einsum('bhde,bhen->bhdn', attn, v).reshape(B, C, N)
        wp = std_weight(proj_w, proj_gain)
        out = jnp.einsum('oc,bcn->bon', wp, out) + proj_b[None, :, None]
        return x + out.reshape(B, C, H, W)

    def _gn(v, G=32, eps=1e-5):
        B_, C_, H_, W_ = v.shape
        g = v.reshape(B_, G, C_ // G, H_, W_)
        m = jnp.mean(g, axis=(2, 3, 4), keepdims=True)
        s = jnp.var(g, axis=(2, 3, 4), keepdims=True)
        return ((g - m) / jnp.sqrt(s + eps)).reshape(v.shape)

    def _ln_c(v, eps=1e-6):
        m = jnp.mean(v, axis=1, keepdims=True)
        s = jnp.var(v, axis=1, keepdims=True)
        return (v - m) / jnp.sqrt(s + eps)

    def _ln_t(v, eps=1e-5):
        m = jnp.mean(v, axis=-1, keepdims=True)
        s = jnp.var(v, axis=-1, keepdims=True)
        return (v - m) / jnp.sqrt(s + eps)

    def _to_tokens(v):
        B_, C_, H_, W_ = v.shape
        return v.reshape(B_, C_, H_ * W_).transpose(0, 2, 1)
    def _from_tokens(t, like):
        B_, C_, H_, W_ = like.shape
        return t.transpose(0, 2, 1).reshape(B_, C_, H_, W_)

    x = _L0_conv_ref(x, L0_conv_qkv_w, L0_conv_qkv_b, L0_conv_qkv_gain, L0_conv_proj_w, L0_conv_proj_b, L0_conv_proj_gain, L0_conv_temperature)
    return x


_drawn_inputs = setup_inputs


def setup_inputs(seed=0):
    import zlib

    import numpy as np

    out = dict(_drawn_inputs(seed))
    spreads = {'L0_conv_qkv_b': (0.0, 0.7),
     'L0_conv_qkv_gain': (1.0, 0.2),
     'L0_conv_proj_b': (0.0, 0.1),
     'L0_conv_proj_gain': (1.0, 0.2),
     'L0_conv_temperature': (1.0, 0.6)}
    factors = {}
    for name, (base, spread) in spreads.items():
        noise = np.random.default_rng([zlib.crc32(name.encode()), seed]).standard_normal(out[name].shape)
        drawn = base * np.exp(spread * noise) if base else spread * noise
        out[name] = jnp.asarray(drawn.astype(out[name].dtype))
    for name, factor in factors.items():
        out[name] = (out[name] * factor).astype(out[name].dtype)
    return out
```

```python
import concourse.bass as bass
from concourse import mybir
from concourse.alu_op_type import AluOpType as ALU
from contextlib import ExitStack



def channel_attention(nc, x, qkv_w, qkv_b, qkv_gain, proj_w, proj_b, proj_gain, temperature, out):
    F32, F32R = mybir.dt.float32, mybir.dt.float32r
    ACT, AX = mybir.ActivationFunctionType, mybir.AxisListType

    P = 128
    BATCH, C, N = x.shape
    HEADS = temperature.shape[0]
    DH = C // HEADS
    CB = C // P
    HPB = P // DH
    QK = 2 * CB
    WB = 4 * CB
    EPS_STD, EPS_L2 = 1e-6, 1e-12
    MASKED = -1e30
    assert CB == 2 and BATCH % 2 == 0 and BATCH >= 6

    UNIT = 2 * P
    UNITS = (N + UNIT - 1) // UNIT
    LAST = N - (UNITS - 1) * UNIT
    assert 0 < LAST <= P
    RING = 3
    TILES = 7
    TN = N // TILES
    PIECES = 4
    PN = N // PIECES
    LAG = 2
    assert TN * TILES == N and PN * PIECES == N and TN % 2 == 0 and TN <= 512
    GC = C + 2

    def ceil_div(a, b):
        return (a + b - 1) // b

    ctx = ExitStack()
    with ctx:
        def sb(name, shape, dt=F32):
            return ctx.enter_context(nc.sbuf_tensor(name, shape, dt))

        def bank(name):
            return ctx.enter_context(nc.psum_tensor(name, [P, 512], F32))

        def sem(name):
            return ctx.enter_context(nc.semaphore(name))

        X = [sb(f"x{k}", [P, CB, N]) for k in range(2)]
        XH = [sb(f"x_high{k}", [P, CB, N], F32R) for k in range(2)]
        XL = [sb(f"x_low{k}", [P, CB, N], F32R) for k in range(2)]
        XT = [sb(f"xT{r}", [P, 2, 2 * C], F32R) for r in range(RING)]

        ident = sb("ident", [P, P])
        mask = sb("mask", [P, P])
        w_nat = sb("w_nat", [P, WB, C])
        w_sq = sb("w_sq", [P, C])
        w_gain = sb("w_gain", [P, WB])
        w_mean = sb("w_mean", [P, WB])
        w_var = sb("w_var", [P, WB])
        w_rstd = sb("w_rstd", [P, WB])
        w_scale = sb("w_scale", [P, WB])
        bias = sb("bias", [P, WB])
        wqkT = sb("wqkT", [P, CB, QK * P])
        wpT = sb("wpT", [P, CB, C])
        w_aug = sb("w_aug", [P, QK, C + 1])
        nb = sb("nb", [P, QK])
        nbb = sb("nbb", [P, QK])
        bq_row = sb("bq_row", [P, C])
        bk_row = sb("bk_row", [P, C])
        temp = sb("temp", [P, CB])
        half = sb("half", [P, WB])

        s_part = sb("s_part", [P, CB, PIECES])
        ga = sb("ga", [P, 4 * P])
        gb = sb("gb", [P, 3 * P])
        g_top = sb("g_top", [P, 2 * P])
        g_low = sb("g_low", [P, P])
        G = sb("G", [P, CB, GC])
        T = sb("T", [P, QK, GC])
        t_junk = sb("t_junk", [P, C + 1])
        n_sq = sb("n_sq", [P, QK])
        n_cl = sb("n_cl", [P, QK])
        r_n = sb("r_n", [P, QK])
        q_scale = sb("q_scale", [P, CB])
        q_sum = sb("q_sum", [P, CB])
        tqT = sb("tqT", [P, CB, C])
        logit0 = sb("logit0", [P, CB, P])
        logit1 = sb("logit1", [P, CB, P])
        logits = sb("logits", [P, CB, P])
        neg_max = sb("neg_max", [P, CB])
        e_attn = sb("e_attn", [P, CB, P])
        e_sum = sb("e_sum", [P, CB])
        r_sum = sb("r_sum", [P, CB])
        attn = sb("attn", [P, CB, P])
        pa = sb("pa", [P, CB, C])
        MH = sb("m_high", [P, CB, C], F32R)
        ML = sb("m_low", [P, CB, C], F32R)
        c_out = sb("c_out", [P, CB])

        tbank = [bank(f"t_bank{r}") for r in range(RING)]
        bankA, bankB = bank("gram_bank0"), bank("gram_bank1")
        obank = [bank("out_bank0"), bank("out_bank1")]
        sbank = bank("small_bank")

        weights_in = sem("weights_in")
        columns_in = sem("columns_in")
        ident_made = sem("ident_made")
        pool_made = sem("pool_made")
        var_ready = sem("var_ready")
        rstd_ready = sem("rstd_ready")
        prep_dve = sem("prep_dve")
        w_ready = sem("w_ready")
        wT_ready = sem("wT_ready")
        wT_copied = sem("wT_copied")
        loaded = [[sem(f"loaded{k}_{t}") for t in range(TILES)] for k in range(2)]
        stored = [[sem(f"stored{k}_{t}") for t in range(TILES)] for k in range(2)]
        xT_ready = sem("xT_ready")
        xT_high = sem("xT_high")
        xT_low = sem("xT_low")
        unit_used = sem("unit_used")
        gram_copied = sem("gram_copied")
        top_ready = sem("top_ready")
        gT_ready = sem("gT_ready")
        g_ready = sem("g_ready")
        t_ready = sem("t_ready")
        t_copied = sem("t_copied")
        tqT_ready = sem("tqT_ready")
        tqT_copied = sem("tqT_copied")
        n_ready = sem("n_ready")
        r_ready = sem("r_ready")
        s_ready = sem("s_ready")
        logits_ready = sem("logits_ready")
        exp_done = sem("exp_done")
        attn_ready = sem("attn_ready")
        pa_ready = sem("pa_ready")
        pa_copied = sem("pa_copied")
        m_ready = sem("m_ready")
        mh_ready = sem("mh_ready")
        ml_ready = sem("ml_ready")
        dve_chain = sem("dve_chain")
        x_high = sem("x_high")
        x_low = sem("x_low")
        o_ready = sem("o_ready")
        o_taken = sem("o_taken")

        def unit_pixels(u):
            return LAST if u == UNITS - 1 else UNIT

        def chunk_rows(u):
            return slice(P - LAST, P) if u == UNITS - 1 else slice(0, P)

        def tiles_for(pixels):
            return ceil_div(pixels, TN)

        def uses(b, par):
            return 16 * (b // 2 + 1) if isinstance(b, int) else (b - par) * 8 + 16

        def each_batch(engine, first, step, last):
            first(0, 0)
            with engine.Fori(1, BATCH - 1, 2) as i:
                step(i, 1)
                step(i + 1, 0)
            last(BATCH - 1, 1)

        block = ctx.enter_context(nc.Block())

        @block.sync
        def _(sp):
            def load(b, par, t):
                sp.dma_start(X[par][:, :, t * TN:(t + 1) * TN],
                             x[b, :, t * TN:(t + 1) * TN].rearrange("(k p) n -> p k n", p=P)
                             ).then_inc(loaded[par][t], 16)

            def store(b, par, t):
                sp.wait_ge(o_taken, b * (CB * TILES) + CB * (t + 1))
                sp.dma_start(out[b, :, t * TN:(t + 1) * TN].rearrange("(k p) n -> p k n", p=P),
                             X[par][:, :, t * TN:(t + 1) * TN]).then_inc(stored[par][t], 16)

            def reload(b, par, t):
                sp.wait_ge(stored[par][t], uses(b, par))
                load(b + 2, par, t)

            def store_tiles(b, par, then_load):
                for t in range(TILES):
                    store(b, par, t)
                    if then_load and t >= LAG:
                        reload(b, par, t - LAG)
                for t in range(TILES - LAG, TILES):
                    if then_load:
                        reload(b, par, t)

            for t in range(TILES):
                load(0, 0, t)
            sp.dma_start(w_nat[:, 0:3 * CB, :], qkv_w.rearrange("(t p) c -> p t c", p=P)).then_inc(weights_in, 16)
            sp.dma_start(w_nat[:, 3 * CB:WB, :], proj_w.rearrange("(t p) c -> p t c", p=P)).then_inc(weights_in, 16)
            for row, n0 in ((bq_row, 0), (bk_row, C)):
                sp.dma_start(row[:, :], qkv_b[n0:n0 + C].rearrange("(a n) -> a n", a=1).to_broadcast([P, C])
                             ).then_inc(weights_in, 16)
            for t in range(TILES):
                load(1, 1, t)
            store_tiles(0, 0, True)
            with sp.Fori(1, BATCH - 3, 2) as i:
                store_tiles(i, 1, True)
                store_tiles(i + 1, 0, True)
            store_tiles(BATCH - 3, 1, True)
            store_tiles(BATCH - 2, 0, False)
            store_tiles(BATCH - 1, 1, False)
            for par in range(2):
                for t in range(TILES):
                    sp.wait_ge(stored[par][t], 16 * (BATCH // 2))

        @block.gpsimd
        def _(pool):
            with nc.allow_non_contiguous_dma(reason="columns of biases, gains and temperatures, once"):
                pool.dma_start(w_gain[:, 0:3 * CB], qkv_gain.rearrange("(t p) -> p t", p=P)).then_inc(columns_in, 16)
                pool.dma_start(w_gain[:, 3 * CB:WB], proj_gain.rearrange("(t p) -> p t", p=P)).then_inc(columns_in, 16)
                pool.dma_start(bias[:, 0:3 * CB], qkv_b.rearrange("(t p) -> p t", p=P)).then_inc(columns_in, 16)
                pool.dma_start(bias[:, 3 * CB:WB], proj_b.rearrange("(t p) -> p t", p=P)).then_inc(columns_in, 16)
                for h in range(HEADS):
                    j, q = h // HPB, h % HPB
                    pool.dma_start(temp[q * DH:(q + 1) * DH, j:j + 1],
                                   temperature[h, :, :].to_broadcast([DH, 1])).then_inc(columns_in, 16)
            nc.gpsimd.memset(ident[:, :], 0.0).then_inc(pool_made, 1)
            nc.gpsimd.memset(half[:, :], -0.5).then_inc(pool_made, 1)
            nc.gpsimd.memset(G[:, :, C:GC], 0.0).then_inc(pool_made, 1)
            pool.wait_ge(pool_made, 3)
            nc.gpsimd.affine_select(out=ident[:, :], in_=ident[:, :], compare_op=ALU.not_equal, fill=1.0,
                                    base=0, pattern=[[-1, P]], channel_multiplier=1).then_inc(ident_made, 1)
            pool.wait_ge(ident_made, 1)
            pool.wait_ge(var_ready, 1)
            nc.gpsimd.tensor_tensor(w_rstd[:, :], w_var[:, :], half[:, :], ALU.pow).then_inc(rstd_ready, 1)

            def split_low(b, par):
                for k in range(CB):
                    for p in range(PIECES):
                        n = slice(p * PN, (p + 1) * PN)
                        pool.wait_ge(x_high, b * (CB * PIECES) + k * PIECES + p + 1)
                        nc.gpsimd.tensor_tensor(XL[par][:, k, n], X[par][:, k, n],
                                                XH[par][:, k, n].bitcast(F32), ALU.subtract).then_inc(x_low, 1)

            def step(b, par, more=True):
                pool.wait_ge(n_ready, b + 1)
                nc.gpsimd.tensor_tensor(r_n[:, :], n_cl[:, :], half[:, 0:QK], ALU.pow).then_inc(r_ready, 1)
                if more:
                    split_low(b + 1, 1 - par)

            split_low(0, 0)
            each_batch(pool, step, step, lambda b, par: step(b, par, False))

        @block.scalar
        def _(act):
            def split_high(b, par):
                for k in range(CB):
                    for p in range(PIECES):
                        if k == 0:
                            for t in range(tiles_for(p * PN), tiles_for((p + 1) * PN)):
                                act.wait_ge(loaded[par][t], uses(b, par))
                        n = slice(p * PN, (p + 1) * PN)
                        nc.scalar.activation(XH[par][:, k, n], X[par][:, k, n], ACT.Copy,
                                             accum_out=s_part[:, k, p:p + 1]).then_inc(x_high, 1)

            def unit_high(b, u):
                chunks = 1 if u == UNITS - 1 else 2
                rows = chunk_rows(u)
                act.wait_ge(xT_ready, b * UNITS + u + 1)
                if u >= RING:
                    act.wait_ge(unit_used, b * UNITS + u - RING + 1)
                nc.scalar.activation(XT[u % RING][rows, 0:chunks, 0:C],
                                     tbank[u % RING][rows, 0:chunks * C].rearrange("p (k c) -> p k c", c=C),
                                     ACT.Copy).then_inc(xT_high, 1)

            def copy_gram(b):
                act.wait_ge(unit_used, (b + 1) * UNITS)
                nc.scalar.activation(ga[:, :], bankA[:, :], ACT.Copy).then_inc(gram_copied, 1)
                nc.scalar.activation(gb[:, :], bankB[:, 0:3 * P], ACT.Copy).then_inc(gram_copied, 1)

            def copy_t(b, j):
                act.wait_ge(t_ready, b * QK + j + 1)
                src = [obank[0], obank[1], sbank, obank[0]][j]
                nc.scalar.activation(T[:, j, 0:C + 1], src[:, 0:C + 1], ACT.Copy).then_inc(t_copied, 1)

            def exps(b):
                act.wait_ge(logits_ready, b + 1)
                for j in range(CB):
                    nc.scalar.activation(e_attn[:, j, :], logits[:, j, :], ACT.Exp, bias=neg_max[:, j:j + 1],
                                         accum_out=e_sum[:, j:j + 1]).then_inc(exp_done, 1)

            def copy_pa(b):
                act.wait_ge(pa_ready, b + 1)
                nc.scalar.activation(pa[:, :, :], sbank[:, :].rearrange("p (k c) -> p k c", c=C), ACT.Copy
                                     ).then_inc(pa_copied, 1)

            def copy_m(b):
                act.wait_ge(m_ready, b + 1)
                nc.scalar.activation(MH[:, :, :], obank[1][:, :].rearrange("p (k c) -> p k c", c=C), ACT.Copy
                                     ).then_inc(mh_ready, 1)

            small = {1: [lambda b: (copy_t(b, 0), copy_t(b, 1), copy_t(b, 2))], 2: [lambda b: copy_t(b, 3)],
                     7: [exps], 9: [copy_pa], 11: [copy_m]}

            def step(b, par, more=True):
                for u in range(UNITS):
                    if more:
                        if u == 0:
                            unit_high(b + 1, 0)
                            unit_high(b + 1, 1)
                        if u + 2 < UNITS:
                            unit_high(b + 1, u + 2)
                    for f in small.get(u, []):
                        f(b)
                if more:
                    copy_gram(b + 1)
                    split_high(b + 1, 1 - par)

            for k in range(3):
                act.wait_ge(wT_ready, k + 1)
                dst = wqkT[:, k, :] if k < 2 else wpT[:, :, :]
                src = tbank[k][:, :] if k < 2 else tbank[k][:, :].rearrange("p (k c) -> p k c", c=C)
                nc.scalar.activation(dst, src, ACT.Copy).then_inc(wT_copied, 1)
            for u in range(UNITS):
                unit_high(0, u)
            copy_gram(0)
            split_high(0, 0)
            each_batch(act, step, step, lambda b, par: step(b, par, False))

        @block.vector
        def _(dve):
            vec = nc.vector
            done = [0]

            def prep(instruction):
                instruction.then_inc(prep_dve, 1)
                done[0] += 1
                dve.wait_ge(prep_dve, done[0])

            prep(vec.memset(mask[:, :], MASKED))
            for q in range(HPB):
                prep(vec.memset(mask[q * DH:(q + 1) * DH, q * DH:(q + 1) * DH], 0.0))
            dve.wait_ge(weights_in, 16 * 4)
            dve.wait_ge(columns_in, 16 * (4 + HEADS))
            prep(vec.reduce_sum(w_mean[:, :], w_nat[:, :, :], AX.X))
            prep(vec.tensor_scalar(w_mean[:, :], w_mean[:, :], 1.0 / C, None, ALU.mult))
            for t in range(WB):
                prep(vec.tensor_scalar(w_nat[:, t, :], w_nat[:, t, :], w_mean[:, t:t + 1], None, ALU.subtract))
            for t in range(WB):
                prep(vec.tensor_tensor_reduce(out=w_sq[:, :], in0=w_nat[:, t, :], in1=w_nat[:, t, :], scale=1.0,
                                              scalar=0.0, op0=ALU.mult, op1=ALU.add, accum_out=w_var[:, t:t + 1]))
            vec.tensor_scalar(w_var[:, :], w_var[:, :], 1.0 / C, EPS_STD, ALU.mult, ALU.add).then_inc(var_ready, 1)
            prep(vec.tensor_scalar(w_scale[:, :], w_gain[:, :], float(C) ** -0.5, None, ALU.mult))
            dve.wait_ge(rstd_ready, 1)
            prep(vec.tensor_tensor(w_scale[:, :], w_scale[:, :], w_rstd[:, :], ALU.mult))
            for t in range(WB):
                vec.tensor_scalar(w_nat[:, t, :], w_nat[:, t, :], w_scale[:, t:t + 1], None, ALU.mult
                                  ).then_inc(w_ready, 1)
            dve.wait_ge(w_ready, WB)
            for t in range(QK):
                prep(vec.tensor_copy(w_aug[:, t, 0:C], w_nat[:, t, :]))
            prep(vec.tensor_scalar(w_aug[:, :, C], bias[:, 0:QK], 2.0, None, ALU.mult))
            prep(vec.tensor_scalar(nb[:, :], bias[:, 0:QK], float(N), None, ALU.mult))
            prep(vec.tensor_tensor(nbb[:, :], nb[:, :], bias[:, 0:QK], ALU.mult))

            CHAIN = 14

            def unit_low(b, u):
                chunks = 1 if u == UNITS - 1 else 2
                rows = chunk_rows(u)
                tile = XT[u % RING][rows, 0:chunks, :]
                dve.wait_ge(xT_high, b * UNITS + u + 1)
                vec.tensor_tensor(tile[:, :, C:2 * C],
                                  tbank[u % RING][rows, 0:chunks * C].rearrange("p (k c) -> p k c", c=C),
                                  tile[:, :, 0:C].bitcast(F32), ALU.subtract).then_inc(xT_low, 1)

            def gram_top(b):
                dve.wait_ge(gram_copied, 2 * b + 2)
                vec.tensor_tensor(g_top[:, :], ga[:, 0:2 * P], ga[:, 2 * P:4 * P], ALU.add).then_inc(top_ready, 1)
                vec.tensor_tensor(g_low[:, :], gb[:, 0:P], gb[:, 2 * P:3 * P], ALU.add).then_inc(top_ready, 1)

            def gram_whole(b):
                dve.wait_ge(gT_ready, b + 1)
                dve.wait_ge(top_ready, 2 * b + 2)
                dve.wait_ge(x_high, (b + 1) * (CB * PIECES))
                vec.tensor_tensor(G[:, 0, 0:C], g_top[:, :], sbank[:, 0:2 * P], ALU.add).then_inc(g_ready, 1)
                vec.tensor_tensor(G[:, 1, 0:P], gb[:, P:2 * P], sbank[:, 2 * P:3 * P], ALU.add).then_inc(g_ready, 1)
                vec.tensor_tensor(G[:, 1, P:C], g_low[:, :], sbank[:, 3 * P:4 * P], ALU.add).then_inc(g_ready, 1)
                vec.reduce_sum(G[:, :, C:C + 1], s_part[:, :, :], AX.X).then_inc(g_ready, 1)

            def norms(b):
                for j in range(QK):
                    dve.wait_ge(t_copied, b * QK + j + 1)
                    vec.tensor_tensor_reduce(out=t_junk[:, :], in0=T[:, j, 0:C + 1], in1=w_aug[:, j, :], scale=1.0,
                                             scalar=nbb[:, j:j + 1], op0=ALU.mult, op1=ALU.add,
                                             accum_out=n_sq[:, j:j + 1]).then_inc(dve_chain, 1)
                    dve.wait_ge(dve_chain, b * CHAIN + j + 1)
                vec.tensor_scalar(n_cl[:, :], n_sq[:, :], EPS_L2 * EPS_L2, None, ALU.max).then_inc(n_ready, 1)
                vec.tensor_tensor(q_sum[:, :], T[:, 0:CB, C], nb[:, 0:CB], ALU.add).then_inc(dve_chain, 1)

            def finish_tqT(b):
                dve.wait_ge(tqT_ready, b + 1)
                for k in range(CB):
                    vec.scalar_tensor_tensor(tqT[:, k, :], bq_row[:, :], G[:, k, C:C + 1],
                                             sbank[:, k * C:(k + 1) * C], ALU.mult, ALU.add
                                             ).then_inc(tqT_copied, 1)

            def make_logits(b):
                dve.wait_ge(r_ready, b + 1)
                vec.tensor_tensor(q_scale[:, :], r_n[:, 0:CB], temp[:, :], ALU.mult).then_inc(dve_chain, 1)
                dve.wait_ge(s_ready, b + 1)
                dve.wait_ge(dve_chain, b * CHAIN + 6)
                for j in range(CB):
                    vec.scalar_tensor_tensor(logit0[:, j, :], bk_row[:, j * P:(j + 1) * P], q_sum[:, j:j + 1],
                                             obank[0][:, j * P:(j + 1) * P], ALU.mult, ALU.add
                                             ).then_inc(dve_chain, 1)
                dve.wait_ge(dve_chain, b * CHAIN + 8)
                vec.tensor_tensor(logit1[:, :, :], logit0[:, :, :],
                                  obank[1][:, 0:CB * P].rearrange("p (k c) -> p k c", c=P), ALU.mult
                                  ).then_inc(dve_chain, 1)
                dve.wait_ge(dve_chain, b * CHAIN + 9)
                for j in range(CB):
                    vec.scalar_tensor_tensor(logits[:, j, :], logit1[:, j, :], q_scale[:, j:j + 1], mask[:, :],
                                             ALU.mult, ALU.add).then_inc(dve_chain, 1)
                dve.wait_ge(dve_chain, b * CHAIN + 11)
                vec.tensor_reduce(neg_max[:, :], logits[:, :, :], AX.X, ALU.max, negate=True
                                  ).then_inc(logits_ready, 1)

            def normalise(b):
                dve.wait_ge(exp_done, 2 * b + 2)
                vec.reciprocal(r_sum[:, :], e_sum[:, :]).then_inc(dve_chain, 1)
                dve.wait_ge(dve_chain, b * CHAIN + 12)
                for j in range(CB):
                    vec.tensor_scalar(attn[:, j, :], e_attn[:, j, :], r_sum[:, j:j + 1], None, ALU.mult
                                      ).then_inc(attn_ready, 1)

            def split_m(b):
                dve.wait_ge(mh_ready, b + 1)
                vec.tensor_tensor(ML[:, :, :], obank[1][:, :].rearrange("p (k c) -> p k c", c=C),
                                  MH[:, :, :].bitcast(F32), ALU.subtract).then_inc(ml_ready, 1)
                vec.tensor_tensor(c_out[:, :], obank[0][:, 0:CB], bias[:, 3 * CB:WB], ALU.add).then_inc(dve_chain, 2)

            small = {1: [gram_whole], 3: [norms], 4: [finish_tqT], 6: [make_logits], 7: [normalise], 11: [split_m]}

            def step(b, par, more=True):
                for u in range(UNITS):
                    if more:
                        if u == 0:
                            unit_low(b + 1, 0)
                            unit_low(b + 1, 1)
                        if u + 2 < UNITS:
                            unit_low(b + 1, u + 2)
                    for f in small.get(u, []):
                        f(b)
                dve.wait_ge(dve_chain, b * CHAIN + CHAIN)
                for t in range(TILES):
                    for k in range(CB):
                        dve.wait_ge(o_ready, b * (CB * TILES) + t * CB + k + 1)
                        vec.scalar_tensor_tensor(X[par][:, k, t * TN:(t + 1) * TN], obank[k][:, 0:TN],
                                                 c_out[:, k:k + 1], X[par][:, k, t * TN:(t + 1) * TN], ALU.add, ALU.add
                                                 ).then_inc(o_taken, 1)
                    if more and t == 2:
                        gram_top(b + 1)

            for u in range(UNITS):
                unit_low(0, u)
            gram_top(0)
            each_batch(dve, step, step, lambda b, par: step(b, par, False))

        @block.tensor
        def _(pe):
            ten = nc.tensor

            def transpose_unit(b, par, u):
                new = range(tiles_for(u * UNIT), tiles_for(u * UNIT + unit_pixels(u)))
                for t in new:
                    pe.wait_ge(loaded[par][t], uses(b, par))
                if u >= RING:
                    pe.wait_ge(xT_low, b * UNITS + u - RING + 1)
                last = None
                for ch in range(ceil_div(unit_pixels(u), P)):
                    n0 = min(u * UNIT + ch * P, N - P)
                    for k in range(CB):
                        last = ten.transpose(tbank[u % RING][:, (ch * CB + k) * P:(ch * CB + k + 1) * P],
                                             X[par][:, k, n0:n0 + P], ident[:, :])
                last.then_inc(xT_ready, 1)

            def gram_unit(b, u):
                pe.wait_ge(xT_low, b * UNITS + u + 1)
                if u == 0 and not (isinstance(b, int) and b == 0):
                    pe.wait_ge(gram_copied, 2 * b)
                last = None
                for ch in range(ceil_div(unit_pixels(u), P)):
                    xt = XT[u % RING][chunk_rows(u), ch, :]
                    flags = dict(start=(u == 0 and ch == 0), stop=(u == UNITS - 1))
                    ten.matmul(bankA[:, :], xt[:, 0:P], xt, **flags)
                    last = ten.matmul(bankB[:, 0:3 * P], xt[:, P:2 * P], xt[:, P:], **flags)
                last.then_inc(unit_used, 1)

            def gram_transposes(b):
                pe.wait_ge(top_ready, 2 * b + 2)
                parts = [ga[:, 2 * P:3 * P], gb[:, P:2 * P], g_top[:, P:2 * P], gb[:, 2 * P:3 * P]]
                for n, part in enumerate(parts):
                    last = ten.transpose(sbank[:, n * P:(n + 1) * P], part, ident[:, :])
                last.then_inc(gT_ready, 1)

            def project(b, j):
                dst = [obank[0], obank[1], sbank, obank[0]][j]
                for k in range(CB):
                    last = ten.matmul(dst[:, 0:C + 1], wqkT[:, k, j * P:(j + 1) * P], G[:, k, 0:C + 1],
                                      start=(k == 0), stop=(k == CB - 1))
                last.then_inc(t_ready, 1)

            def projections(b):
                pe.wait_ge(g_ready, 4 * b + 4)
                for j in range(3):
                    project(b, j)

            def last_projection(b):
                pe.wait_ge(t_copied, QK * b + 1)
                project(b, 3)

            def tq_transposes(b):
                pe.wait_ge(t_copied, QK * b + 3)
                for k in range(CB):
                    for j in range(CB):
                        last = ten.transpose(sbank[:, k * C + j * P:k * C + (j + 1) * P],
                                             T[:, j, k * P:(k + 1) * P], ident[:, :])
                last.then_inc(tqT_ready, 1)

            def scores(b):
                pe.wait_ge(r_ready, b + 1)
                for j in range(CB):
                    ten.transpose(obank[1][:, j * P:(j + 1) * P],
                                  r_n[:, CB + j:CB + j + 1].to_broadcast([P, P]), ident[:, :])
                pe.wait_ge(tqT_copied, CB * b + CB)
                for j in range(CB):
                    for k in range(CB):
                        last = ten.matmul(obank[0][:, j * P:(j + 1) * P], tqT[:, k, j * P:(j + 1) * P],
                                          wqkT[:, k, C + j * P:C + (j + 1) * P], start=(k == 0), stop=(k == CB - 1))
                last.then_inc(s_ready, 1)

            def project_attn(b):
                pe.wait_ge(attn_ready, 2 * b + 2)
                for j in range(CB):
                    last = ten.matmul(sbank[:, j * C:(j + 1) * C], attn[:, j, :], wpT[:, j, :], start=True, stop=True)
                last.then_inc(pa_ready, 1)

            def whole_map(b):
                pe.wait_ge(pa_copied, b + 1)
                for k in range(CB):
                    for j in range(CB):
                        ten.matmul(obank[1][:, k * C:(k + 1) * C], w_nat[:, QK + j, k * P:(k + 1) * P], pa[:, j, :],
                                   start=(j == 0), stop=(j == CB - 1))
                for k in range(CB):
                    for j in range(CB):
                        last = ten.matmul(obank[0][:, k:k + 1], pa[:, j, k * P:(k + 1) * P],
                                          bias[:, QK + j:QK + j + 1], start=(j == 0), stop=(j == CB - 1))
                last.then_inc(m_ready, 1)

            def output(b, par):
                pe.wait_ge(ml_ready, b + 1)
                pe.wait_ge(dve_chain, b * 14 + 14)
                pe.wait_ge(x_low, (b + 1) * (CB * PIECES))
                for t in range(TILES):
                    n = slice(t * TN, (t + 1) * TN)
                    for o in range(CB):
                        if t > 0:
                            pe.wait_ge(o_taken, b * (CB * TILES) + (t - 1) * CB + o + 1)
                        cols = slice(o * P, (o + 1) * P)
                        terms = [(m, v, k) for k in range(CB) for m, v in ((MH, XH), (MH, XL), (ML, XH))]
                        for i, (m, v, k) in enumerate(terms):
                            last = ten.matmul(obank[o][:, 0:TN], m[:, k, cols], v[par][:, k, n],
                                              start=(i == 0), stop=(i == len(terms) - 1))
                        last.then_inc(o_ready, 1)

            small = {0: [gram_transposes], 1: [projections], 2: [last_projection], 4: [tq_transposes],
                     6: [scores], 9: [project_attn], 11: [whole_map]}

            def step(b, par, more=True):
                for u in range(UNITS):
                    if more:
                        if u == 0:
                            transpose_unit(b + 1, 1 - par, 0)
                            transpose_unit(b + 1, 1 - par, 1)
                        if u + 2 < UNITS:
                            transpose_unit(b + 1, 1 - par, u + 2)
                        gram_unit(b + 1, u)
                    for f in small.get(u, []):
                        f(b)
                output(b, par)

            pe.wait_ge(w_ready, WB)
            pe.wait_ge(ident_made, 1)
            for k in range(CB):
                for j in range(QK):
                    last = ten.transpose(tbank[k][:, j * P:(j + 1) * P], w_nat[:, j, k * P:(k + 1) * P], ident[:, :])
                last.then_inc(wT_ready, 1)
            for j in range(CB):
                for o in range(CB):
                    last = ten.transpose(tbank[2][:, j * C + o * P:j * C + (o + 1) * P],
                                         w_nat[:, 3 * CB + o, j * P:(j + 1) * P], ident[:, :])
            last.then_inc(wT_ready, 1)
            pe.wait_ge(wT_copied, 3)
            transpose_unit(0, 0, 0)
            transpose_unit(0, 0, 1)
            for u in range(UNITS):
                if u + 2 < UNITS:
                    transpose_unit(0, 0, u + 2)
                gram_unit(0, u)
            each_batch(pe, step, step, lambda b, par: step(b, par, False))


def kernel(**inputs):
    import numpy as np
    import concourse.bacc as bacc
    from concourse.bass_utils import run_bass_kernel_spmd

    nc = bacc.Bacc("TRN2", target_bir_lowering=False, num_devices=1)
    names = ["x", "L0_conv_qkv_w", "L0_conv_qkv_b", "L0_conv_qkv_gain", "L0_conv_proj_w", "L0_conv_proj_b",
             "L0_conv_proj_gain", "L0_conv_temperature"]
    shape = inputs["x"].shape
    arrays, args = {}, []
    for name in names:
        a = np.ascontiguousarray(inputs[name])
        if name == "x":
            a = a.reshape(shape[0], shape[1], shape[2] * shape[3])
        arrays[f"in_{name}"] = a
        args.append(nc.dram_tensor(f"in_{name}", a.shape, mybir.dt.from_np(a.dtype), kind="ExternalInput").ap())
    out = nc.dram_tensor("out", arrays["in_x"].shape, mybir.dt.float32, kind="ExternalOutput").ap()
    channel_attention(nc, *args, out)
    r = run_bass_kernel_spmd(nc, [arrays], core_ids=[0])
    return r.results[0]["out"].reshape(shape)
```

```python
import concourse.bass as bass
from concourse import mybir
from concourse.alu_op_type import AluOpType as ALU
from contextlib import ExitStack



def channel_attention(nc, x, qkv_w, qkv_b, qkv_gain, proj_w, proj_b, proj_gain, temperature, out):
    F32, F32R = mybir.dt.float32, mybir.dt.float32r
    ACT, AX = mybir.ActivationFunctionType, mybir.AxisListType

    P = 128
    BATCH, C, N = x.shape
    HEADS = temperature.shape[0]
    DH = C // HEADS
    CB = C // P
    HPB = P // DH
    QK = 2 * CB
    WB = 4 * CB
    EPS_STD, EPS_L2 = 1e-6, 1e-12
    MASKED = -1e30
    assert CB == 2 and BATCH % 2 == 0 and BATCH >= 6 and P // DH == 4

    Q = 32
    NQ = P // Q
    UNIT = 2 * P
    FULL = N // UNIT
    R = FULL * UNIT // NQ
    LAST = N - FULL * UNIT
    UNITS = FULL + 1
    assert 0 < LAST <= P
    RING = 4
    FIRST = 2
    AHEAD = RING
    TILES = 7
    TN = N // TILES
    SPLITS = [(0, 2), (2, 4), (4, 6), (6, 7)]
    OUTS = 3
    OBANKS = 3
    assert SPLITS[-1][1] == TILES and TN * TILES == N and TN % 2 == 0 and TN <= 512
    GC = C + 2

    def ceil_div(a, b):
        return (a + b - 1) // b

    ctx = ExitStack()
    with ctx:
        def sb(name, shape, dt=F32):
            return ctx.enter_context(nc.sbuf_tensor(name, shape, dt))

        def bank(name):
            return ctx.enter_context(nc.psum_tensor(name, [P, 512], F32))

        def sem(name):
            return ctx.enter_context(nc.semaphore(name))

        X = [sb(f"x{k}", [P, CB, N]) for k in range(2)]
        XH = sb("x_high", [P, CB, N], F32R)
        XL = sb("x_low", [P, CB, N], F32R)
        OT = [sb(f"out_tile{k}", [P, CB, TN]) for k in range(OUTS)]
        Y = sb("x_quads", [P, C // Q, R])
        YT = sb("x_turned", [P, FULL, 2 * C])
        XT = [sb(f"xT{r}", [P, 2, 2 * C], F32R) for r in range(RING)]

        ident = sb("ident", [P, P])
        mask = sb("mask", [P, P])
        w_nat = sb("w_nat", [P, WB, C + 1])
        w_gain = sb("w_gain", [P, WB])
        w_mean = sb("w_mean", [P, WB])
        w_var = sb("w_var", [P, WB])
        w_rstd = sb("w_rstd", [P, WB])
        w_scale = sb("w_scale", [P, WB])
        bias = sb("bias", [P, WB])
        wqkT = sb("wqkT", [P, CB, QK * P])
        wqkT_h = sb("wqkT_high", [P, CB, QK * P], F32R)
        wqkT_l = sb("wqkT_low", [P, CB, QK * P], F32R)
        wpT = sb("wpT", [P, CB, C])
        nb = sb("nb", [P, QK])
        nbb = sb("nbb", [P, QK])
        bq_row = sb("bq_row", [P, C])
        bk_row = sb("bk_row", [P, C])
        bv_row = sb("bv_row", [P, C])
        eye = sb("eye", [P, CB, C])
        temp = sb("temp", [P, CB])
        half = sb("half", [P, WB])

        s_part = sb("s_part", [P, CB, len(SPLITS)])
        ga = sb("ga", [P, 4 * P])
        junk = ga
        gb = sb("gb", [P, 3 * P])
        g_top = sb("g_top", [P, 2 * P])
        g_low = sb("g_low", [P, P])
        G = sb("G", [P, CB, GC])
        m_full = G[:, :, 0:C]
        GH = sb("G_high", [P, CB, GC], F32R)
        GL = sb("G_low", [P, CB, GC], F32R)
        T = sb("T", [P, CB, GC])
        n_sq = sb("n_sq", [P, QK])
        n_cl = sb("n_cl", [P, QK])
        r_n = sb("r_n", [P, QK])
        q_scale = sb("q_scale", [P, CB])
        q_sum = sb("q_sum", [P, CB])
        tqT = sb("tqT", [P, CB, C])
        logits = sb("logits", [P, CB, P])
        neg_max = sb("neg_max", [P, CB])
        e_sum = sb("e_sum", [P, CB])
        r_sum = sb("r_sum", [P, CB])
        attn = sb("attn", [P, CB, P])
        pa = tqT
        av = sb("av", [P, CB])
        MH = sb("m_high", [P, CB, C], F32R)
        ML = sb("m_low", [P, CB, C], F32R)
        c_out = sb("c_out", [P, CB])

        bankA, bankB = bank("gram_bank0"), bank("gram_bank1")
        lbank = bank("last_unit_bank")
        sbank = [bank("small_bank0"), bank("small_bank1")]
        obank = [bank(f"out_bank{k}") for k in range(OBANKS)]

        weights_in = sem("weights_in")
        columns_in = sem("columns_in")
        ident_made = sem("ident_made")
        pool_made = sem("pool_made")
        var_ready = sem("var_ready")
        rstd_ready = sem("rstd_ready")
        prep_dve = sem("prep_dve")
        w_ready = sem("w_ready")
        wT_ready = sem("wT_ready")
        wT_copied = sem("wT_copied")
        loaded = [[sem(f"loaded{k}_{t}") for t in range(TILES)] for k in range(2)]
        quads_in = [sem(f"quads_in{i}") for i in range(NQ)]
        stored = [sem(f"stored{k}") for k in range(OUTS)]
        last_ready = sem("last_ready")
        quads_used = sem("quads_used")
        xT_high = sem("xT_high")
        xT_low = sem("xT_low")
        unit_used = sem("unit_used")
        gram_copied = sem("gram_copied")
        top_ready = sem("top_ready")
        gT_ready = sem("gT_ready")
        g_ready = sem("g_ready")
        sums_ready = sem("sums_ready")
        gh_ready = sem("gh_ready")
        gl_ready = sem("gl_ready")
        t_ready = sem("t_ready")
        t_copied = sem("t_copied")
        tqT_ready = sem("tqT_ready")
        tqT_copied = sem("tqT_copied")
        n_ready = sem("n_ready")
        r_ready = sem("r_ready")
        s_ready = sem("s_ready")
        logits_ready = sem("logits_ready")
        exp_done = sem("exp_done")
        attn_ready = sem("attn_ready")
        av_ready = sem("av_ready")
        av_spread = sem("av_spread")
        c_ready = sem("c_ready")
        pa_ready = sem("pa_ready")
        pa_copied = sem("pa_copied")
        m_ready = sem("m_ready")
        m_whole = sem("m_whole")
        mh_ready = sem("mh_ready")
        ml_ready = sem("ml_ready")
        qsum_ready = sem("qsum_ready")
        dve_chain = sem("dve_chain")
        x_high = sem("x_high")
        x_low = sem("x_low")
        o_ready = sem("o_ready")
        o_taken = [sem(f"o_taken{k}") for k in range(CB)]

        def chunk_rows(u):
            return slice(P - LAST, P) if u == FULL else slice(0, P)

        def unit_chunks(u):
            return 1 if u == FULL else 2

        def unit_source(u):
            whole = lbank[chunk_rows(u), 0:C] if u == FULL else YT[:, u, :]
            return whole.rearrange("p (k c) -> p k c", c=C)

        def tiles_for(pixels):
            return (pixels + TN - 1) // TN

        def uses(b, par):
            return 16 * (b // 2 + 1) if isinstance(b, int) else (b - par) * 8 + 16

        def out_uses(t):
            return len(range(t % OUTS, TILES, OUTS)), t // OUTS

        def each_batch(engine, step):
            step(0, 0, True, True)
            with engine.Fori(1, BATCH - 3, 2) as i:
                step(i, 1, True, True)
                step(i + 1, 0, True, True)
            step(BATCH - 3, 1, True, True)
            step(BATCH - 2, 0, True, False)
            step(BATCH - 1, 1, False, False)

        TOP_AT, TRANSPOSES_AT, WHOLE_AT, HIGH_AT, LOW_AT = 1, 2, 3, 4, 5
        T_BANKS = [sbank[0], sbank[1], obank[0], obank[1]]

        def out_free(engine, b, t):
            count, place = out_uses(t)
            if not isinstance(b, int) or b > 0 or place > 0:
                engine.wait_ge(stored[t % OUTS], (b * count + place) * 16)

        block = ctx.enter_context(nc.Block())

        @block.sync
        def _(sp):
            def load(b, par, t):
                sp.dma_start(X[par][:, :, t * TN:(t + 1) * TN],
                             x[b, :, t * TN:(t + 1) * TN].rearrange("(k p) n -> p k n", p=P)
                             ).then_inc(loaded[par][t], 16)

            def gather(b, par):
                for i in range(NQ):
                    for t in range(tiles_for(i * R), tiles_for((i + 1) * R)):
                        sp.wait_ge(loaded[par][t], uses(b, par))
                    for q in range(NQ):
                        sp.dma_start(Y[i * Q:(i + 1) * Q, q:C // Q:NQ, :],
                                     X[par][q * Q:(q + 1) * Q, :, i * R:(i + 1) * R]).then_inc(quads_in[i], 16)

            def step(b, par, following, after):
                if after:
                    for m, tiles in enumerate(SPLITS):
                        sp.wait_ge(x_low, b * (CB * len(SPLITS)) + CB * (m + 1))
                        for t in range(*tiles):
                            load(b + 2, par, t)
                    sp.wait_ge(quads_used, (b + 2) * FULL)
                    gather(b + 2, par)
                for t in range(TILES):
                    for k in range(CB):
                        sp.wait_ge(o_taken[k], b * TILES + t + 1)
                    sp.dma_start(out[b, :, t * TN:(t + 1) * TN].rearrange("(k p) n -> p k n", p=P),
                                 OT[t % OUTS][:, :, :]).then_inc(stored[t % OUTS], 16)

            for t in range(TILES):
                load(0, 0, t)
            sp.dma_start(w_nat[:, 0:3 * CB, 0:C], qkv_w.rearrange("(t p) c -> p t c", p=P)).then_inc(weights_in, 16)
            sp.dma_start(w_nat[:, 3 * CB:WB, 0:C], proj_w.rearrange("(t p) c -> p t c", p=P)).then_inc(weights_in, 16)
            for row, n0 in ((bq_row, 0), (bk_row, C), (bv_row, 2 * C)):
                sp.dma_start(row[:, :], qkv_b[n0:n0 + C].rearrange("(a n) -> a n", a=1).to_broadcast([P, C])
                             ).then_inc(weights_in, 16)
            gather(0, 0)
            for t in range(TILES):
                load(1, 1, t)
            sp.wait_ge(quads_used, FULL)
            gather(1, 1)
            each_batch(sp, step)
            for k in range(OUTS):
                sp.wait_ge(stored[k], 16 * BATCH * out_uses(k)[0])

        @block.gpsimd
        def _(pool):
            nc.gpsimd.memset(ident[:, :], 0.0).then_inc(pool_made, 1)
            nc.gpsimd.memset(half[:, :], -0.5).then_inc(pool_made, 1)
            nc.gpsimd.memset(G[:, :, C:GC], 0.0).then_inc(pool_made, 1)
            pool.wait_ge(pool_made, 3)
            nc.gpsimd.affine_select(out=ident[:, :], in_=ident[:, :], compare_op=ALU.not_equal, fill=1.0,
                                    base=0, pattern=[[-1, P]], channel_multiplier=1).then_inc(ident_made, 1)
            pool.wait_ge(ident_made, 1)
            pool.wait_ge(var_ready, 1)
            nc.gpsimd.tensor_tensor(w_rstd[:, :], w_var[:, :], half[:, :], ALU.pow).then_inc(rstd_ready, 1)

            def split_low(b, par, m):
                n = slice(SPLITS[m][0] * TN, SPLITS[m][1] * TN)
                for k in range(CB):
                    pool.wait_ge(x_high, b * (CB * len(SPLITS)) + CB * m + k + 1)
                    nc.gpsimd.tensor_tensor(XL[:, k, n], X[par][:, k, n], XH[:, k, n].bitcast(F32), ALU.subtract
                                            ).then_inc(x_low, 1)

            def step(b, par, following, after):
                pool.wait_ge(n_ready, b + 1)
                nc.gpsimd.tensor_tensor(r_n[:, :], n_cl[:, :], half[:, 0:QK], ALU.pow).then_inc(r_ready, 1)
                if following:
                    for m in range(len(SPLITS)):
                        split_low(b + 1, 1 - par, m)

            for m in range(len(SPLITS)):
                split_low(0, 0, m)
            each_batch(pool, step)

        @block.scalar
        def _(act):
            def split_high(b, par, m):
                for t in range(*SPLITS[m]):
                    act.wait_ge(loaded[par][t], uses(b, par))
                n = slice(SPLITS[m][0] * TN, SPLITS[m][1] * TN)
                for k in range(CB):
                    nc.scalar.activation(XH[:, k, n], X[par][:, k, n], ACT.Copy,
                                         accum_out=s_part[:, k, m:m + 1]).then_inc(x_high, 1)

            def unit_high(b, u):
                if u == FULL:
                    act.wait_ge(last_ready, b + 1)
                else:
                    act.wait_ge(quads_used, b * FULL + u + 1)
                if u >= RING:
                    act.wait_ge(unit_used, b * UNITS + u - RING + 1)
                nc.scalar.activation(XT[u % RING][chunk_rows(u), 0:unit_chunks(u), 0:C], unit_source(u), ACT.Copy
                                     ).then_inc(xT_high, 1)

            def copy_gram(b):
                act.wait_ge(unit_used, (b + 1) * UNITS)
                nc.scalar.activation(ga[:, :], bankA[:, :], ACT.Copy).then_inc(gram_copied, 1)
                nc.scalar.activation(gb[:, :], bankB[:, 0:3 * P], ACT.Copy).then_inc(gram_copied, 1)

            def gram_high(b):
                act.wait_ge(g_ready, 3 * b + 3)
                nc.scalar.activation(GH[:, :, 0:C], G[:, :, 0:C], ACT.Copy).then_inc(gh_ready, 1)

            def copy_t(b):
                for j in range(CB):
                    act.wait_ge(t_ready, b * QK + j + 1)
                    nc.scalar.activation(T[:, j, :], T_BANKS[j][:, 0:GC], ACT.Copy).then_inc(t_copied, 1)

            def exps(b):
                act.wait_ge(logits_ready, b + 1)
                for j in range(CB):
                    nc.scalar.activation(attn[:, j, :], logits[:, j, :], ACT.Exp, bias=neg_max[:, j:j + 1],
                                         accum_out=e_sum[:, j:j + 1]).then_inc(exp_done, 1)

            def copy_pa(b):
                act.wait_ge(pa_ready, b + 1)
                nc.scalar.activation(pa[:, :, :], obank[2][:, :].rearrange("p (k c) -> p k c", c=C), ACT.Copy
                                     ).then_inc(pa_copied, 1)

            def map_high(b):
                act.wait_ge(m_whole, b + 1)
                nc.scalar.activation(MH[:, :, :], m_full, ACT.Copy).then_inc(mh_ready, 1)

            small = {AHEAD - 1: [copy_t], 8: [exps], 12: [copy_pa, map_high]}

            def step(b, par, following, after):
                for u in range(AHEAD - 1, UNITS):
                    if following and u >= AHEAD:
                        unit_high(b + 1, u)
                    for f in small.get(u, []):
                        f(b)
                if following:
                    copy_gram(b + 1)
                act.wait_ge(c_ready, CB * b + CB)
                for t in range(TILES):
                    act.wait_ge(o_ready, b * (CB * TILES) + t * CB + 1)
                    out_free(act, b, t)
                    nc.scalar.activation(OT[t % OUTS][:, 0, :], obank[t * CB % OBANKS][:, 0:TN], ACT.Identity,
                                         bias=c_out[:, 0:1]).then_inc(o_taken[0], 1)
                    for m, (_, end) in enumerate(SPLITS):
                        if following and end == t + 1:
                            act.wait_ge(o_ready, b * (CB * TILES) + CB * end)
                            split_high(b + 1, 1 - par, m)
                    if following and t == HIGH_AT:
                        gram_high(b + 1)
                    if after and t >= TILES - AHEAD:
                        unit_high(b + 2, t - (TILES - AHEAD))

            with nc.allow_non_contiguous_dma(reason="columns of biases, gains and temperatures, once"):
                act.dma_start(w_gain[:, 0:3 * CB], qkv_gain.rearrange("(t p) -> p t", p=P)).then_inc(columns_in, 16)
                act.dma_start(w_gain[:, 3 * CB:WB], proj_gain.rearrange("(t p) -> p t", p=P)).then_inc(columns_in, 16)
                act.dma_start(bias[:, 0:3 * CB], qkv_b.rearrange("(t p) -> p t", p=P)).then_inc(columns_in, 16)
                act.dma_start(bias[:, 3 * CB:WB], proj_b.rearrange("(t p) -> p t", p=P)).then_inc(columns_in, 16)
                for h in range(HEADS):
                    j, q = h // HPB, h % HPB
                    act.dma_start(temp[q * DH:(q + 1) * DH, j:j + 1],
                                   temperature[h, :, :].to_broadcast([DH, 1])).then_inc(columns_in, 16)
            for k in range(3):
                act.wait_ge(wT_ready, k + 1)
                if k < CB:
                    nc.scalar.activation(wqkT[:, k, :], obank[k][:, :], ACT.Copy).then_inc(wT_copied, 1)
                    act.wait_ge(wT_copied, 2 * k + 1)
                    nc.scalar.activation(wqkT_h[:, k, :], wqkT[:, k, :], ACT.Copy).then_inc(wT_copied, 1)
                else:
                    nc.scalar.activation(wpT[:, :, :], obank[2][:, :].rearrange("p (k c) -> p k c", c=C), ACT.Copy
                                         ).then_inc(wT_copied, 1)
            for u in range(UNITS):
                unit_high(0, u)
            copy_gram(0)
            for m in range(len(SPLITS)):
                split_high(0, 0, m)
            gram_high(0)
            for u in range(AHEAD):
                unit_high(1, u)
            each_batch(act, step)

        @block.vector
        def _(dve):
            vec = nc.vector
            done = [0]

            def prep(instruction):
                instruction.then_inc(prep_dve, 1)
                done[0] += 1
                dve.wait_ge(prep_dve, done[0])

            prep(vec.memset(mask[:, :], MASKED))
            for q in range(HPB):
                prep(vec.memset(mask[q * DH:(q + 1) * DH, q * DH:(q + 1) * DH], 0.0))
            prep(vec.memset(eye[:, :, :], 0.0))
            dve.wait_ge(ident_made, 1)
            for k in range(CB):
                prep(vec.tensor_copy(eye[:, k, k * P:(k + 1) * P], ident[:, :]))
            dve.wait_ge(weights_in, 16 * 5)
            dve.wait_ge(columns_in, 16 * (4 + HEADS))
            prep(vec.reduce_sum(w_mean[:, :], w_nat[:, :, 0:C], AX.X))
            prep(vec.tensor_scalar(w_mean[:, :], w_mean[:, :], 1.0 / C, None, ALU.mult))
            for t in range(WB):
                prep(vec.tensor_scalar(w_nat[:, t, 0:C], w_nat[:, t, 0:C], w_mean[:, t:t + 1], None, ALU.subtract))
            for t in range(WB):
                prep(vec.tensor_tensor_reduce(out=ga[:, 0:C], in0=w_nat[:, t, 0:C], in1=w_nat[:, t, 0:C], scale=1.0,
                                              scalar=0.0, op0=ALU.mult, op1=ALU.add, accum_out=w_var[:, t:t + 1]))
            vec.tensor_scalar(w_var[:, :], w_var[:, :], 1.0 / C, EPS_STD, ALU.mult, ALU.add).then_inc(var_ready, 1)
            prep(vec.tensor_scalar(w_scale[:, :], w_gain[:, :], float(C) ** -0.5, None, ALU.mult))
            dve.wait_ge(rstd_ready, 1)
            prep(vec.tensor_tensor(w_scale[:, :], w_scale[:, :], w_rstd[:, :], ALU.mult))
            for t in range(WB):
                vec.tensor_scalar(w_nat[:, t, 0:C], w_nat[:, t, 0:C], w_scale[:, t:t + 1], None, ALU.mult
                                  ).then_inc(w_ready, 1)
            dve.wait_ge(w_ready, WB)
            prep(vec.tensor_scalar(w_nat[:, 0:QK, C], bias[:, 0:QK], 2.0, None, ALU.mult))
            prep(vec.tensor_scalar(nb[:, :], bias[:, 0:QK], float(N), None, ALU.mult))
            prep(vec.tensor_tensor(nbb[:, :], nb[:, :], bias[:, 0:QK], ALU.mult))

            dve.wait_ge(wT_copied, 2 * CB)
            prep(vec.tensor_tensor(wqkT_l[:, :, :], wqkT[:, :, :], wqkT_h[:, :, :].bitcast(F32), ALU.subtract))

            def turn(b, u):
                if u == 0:
                    for i in range(NQ):
                        dve.wait_ge(quads_in[i], (b + 1) * (16 * NQ))
                    if not isinstance(b, int) or b > 0:
                        dve.wait_ge(xT_low, b * UNITS)
                vec.transpose(YT[:, u, :].rearrange("p (j g a) -> p j g a", j=2, a=Q),
                              Y[:, :, u * 2 * Q:(u + 1) * 2 * Q].rearrange("p g (j a) -> p j g a", a=Q)
                              ).then_inc(quads_used, 1)

            def unit_low(b, u):
                tile = XT[u % RING][chunk_rows(u), 0:unit_chunks(u), :]
                dve.wait_ge(xT_high, b * UNITS + u + 1)
                vec.tensor_tensor(tile[:, :, C:2 * C], unit_source(u), tile[:, :, 0:C].bitcast(F32), ALU.subtract
                                  ).then_inc(xT_low, 1)

            def gram_top(b):
                dve.wait_ge(gram_copied, 2 * b + 2)
                vec.tensor_tensor(g_top[:, :], ga[:, 0:2 * P], ga[:, 2 * P:4 * P], ALU.add).then_inc(top_ready, 1)
                vec.tensor_tensor(g_low[:, :], gb[:, 0:P], gb[:, 2 * P:3 * P], ALU.add).then_inc(top_ready, 1)

            def gram_whole(b):
                dve.wait_ge(gT_ready, b + 1)
                dve.wait_ge(top_ready, 2 * b + 2)
                vec.tensor_tensor(G[:, 0, 0:C], g_top[:, :], sbank[0][:, 0:2 * P], ALU.add).then_inc(g_ready, 1)
                vec.tensor_tensor(G[:, 1, 0:P], gb[:, P:2 * P], sbank[0][:, 2 * P:3 * P], ALU.add).then_inc(g_ready, 1)
                vec.tensor_tensor(G[:, 1, P:C], g_low[:, :], sbank[0][:, 3 * P:4 * P], ALU.add).then_inc(g_ready, 1)

            def gram_low(b):
                dve.wait_ge(gh_ready, b + 1)
                dve.wait_ge(g_ready, 3 * b + 3)
                vec.tensor_tensor(GL[:, :, 0:C], G[:, :, 0:C], GH[:, :, 0:C].bitcast(F32), ALU.subtract
                                  ).then_inc(gl_ready, 1)

            def sums(b):
                behind = slice(C, GC)
                dve.wait_ge(x_high, (b + 1) * (CB * len(SPLITS)))
                vec.reduce_sum(G[:, :, C:C + 1], s_part[:, :, :], AX.X).then_inc(sums_ready, 1)
                dve.wait_ge(sums_ready, 3 * b + 1)
                vec.tensor_copy(GH[:, :, behind], G[:, :, behind]).then_inc(sums_ready, 1)
                dve.wait_ge(sums_ready, 3 * b + 2)
                vec.tensor_tensor(GL[:, :, behind], G[:, :, behind], GH[:, :, behind].bitcast(F32), ALU.subtract
                                  ).then_inc(sums_ready, 1)

            CHAIN = 11

            def norms(b, blocks):
                for j in blocks:
                    if j < CB:
                        dve.wait_ge(t_copied, b * CB + j + 1)
                        t_j = T[:, j, :]
                    else:
                        dve.wait_ge(t_ready, b * QK + j + 1)
                        t_j = T_BANKS[j]
                    if j > 0:
                        dve.wait_ge(dve_chain, b * CHAIN + j)
                    vec.tensor_tensor_reduce(out=junk[:, 0:C + 1], in0=t_j[:, 0:C + 1], in1=w_nat[:, j, :], scale=1.0,
                                             scalar=nbb[:, j:j + 1], op0=ALU.mult, op1=ALU.add,
                                             accum_out=n_sq[:, j:j + 1]).then_inc(dve_chain, 1)

            def norms_q(b):
                norms(b, range(CB))
                vec.tensor_tensor(q_sum[:, :], T[:, 0:CB, C], nb[:, 0:CB], ALU.add).then_inc(qsum_ready, 1)

            def norms_k(b):
                norms(b, range(CB, QK))
                dve.wait_ge(dve_chain, b * CHAIN + 4)
                vec.tensor_scalar(n_cl[:, :], n_sq[:, :], EPS_L2 * EPS_L2, None, ALU.max).then_inc(n_ready, 1)

            def finish_tqT(b):
                dve.wait_ge(tqT_ready, b + 1)
                for k in range(CB):
                    vec.scalar_tensor_tensor(tqT[:, k, :], bq_row[:, :], G[:, k, C:C + 1],
                                             obank[2][:, k * C:(k + 1) * C], ALU.mult, ALU.add
                                             ).then_inc(tqT_copied, 1)

            def make_logits(b):
                dve.wait_ge(r_ready, b + 1)
                vec.tensor_tensor(q_scale[:, :], r_n[:, 0:CB], temp[:, :], ALU.mult).then_inc(dve_chain, 1)
                dve.wait_ge(s_ready, b + 1)
                dve.wait_ge(qsum_ready, b + 1)
                for j in range(CB):
                    vec.scalar_tensor_tensor(logits[:, j, :], bk_row[:, j * P:(j + 1) * P], q_sum[:, j:j + 1],
                                             sbank[1][:, j * P:(j + 1) * P], ALU.mult, ALU.add
                                             ).then_inc(dve_chain, 1)
                dve.wait_ge(dve_chain, b * CHAIN + 7)
                vec.tensor_tensor(logits[:, :, :], logits[:, :, :],
                                  sbank[0][:, 0:CB * P].rearrange("p (k c) -> p k c", c=P), ALU.mult
                                  ).then_inc(dve_chain, 1)
                dve.wait_ge(dve_chain, b * CHAIN + 8)
                for j in range(CB):
                    vec.scalar_tensor_tensor(logits[:, j, :], logits[:, j, :], q_scale[:, j:j + 1], mask[:, :],
                                             ALU.mult, ALU.add).then_inc(dve_chain, 1)
                dve.wait_ge(dve_chain, b * CHAIN + 10)
                vec.tensor_reduce(neg_max[:, :], logits[:, :, :], AX.X, ALU.max, negate=True
                                  ).then_inc(logits_ready, 1)

            def normalise(b):
                dve.wait_ge(exp_done, 2 * b + 2)
                vec.reciprocal(r_sum[:, :], e_sum[:, :]).then_inc(dve_chain, 1)
                dve.wait_ge(dve_chain, b * CHAIN + 11)
                for j in range(CB):
                    vec.tensor_scalar(attn[:, j, :], attn[:, j, :], r_sum[:, j:j + 1], None, ALU.mult
                                      ).then_inc(attn_ready, 1)

            def attn_bias(b):
                dve.wait_ge(attn_ready, CB * b + CB)
                for j in range(CB):
                    vec.tensor_tensor_reduce(out=junk[:, j * P:(j + 1) * P], in0=attn[:, j, :],
                                             in1=bv_row[:, j * P:(j + 1) * P], scale=1.0, scalar=0.0,
                                             op0=ALU.mult, op1=ALU.add, accum_out=av[:, j:j + 1]
                                             ).then_inc(av_ready, 1)

            def out_bias(b):
                dve.wait_ge(av_spread, b + 1)
                for o in range(CB):
                    vec.tensor_tensor_reduce(out=junk[:, o * C:(o + 1) * C], in0=sbank[0][:, 0:C],
                                             in1=w_nat[:, 3 * CB + o, 0:C], scale=1.0, scalar=bias[:, 3 * CB + o:3 * CB + o + 1],
                                             op0=ALU.mult, op1=ALU.add, accum_out=c_out[:, o:o + 1]
                                             ).then_inc(c_ready, 1)

            def map_whole(b):
                dve.wait_ge(m_ready, b + 1)
                vec.tensor_tensor(m_full, obank[0][:, :].rearrange("p (k c) -> p k c", c=C), eye[:, :, :],
                                  ALU.add).then_inc(m_whole, 1)

            def map_low(b):
                dve.wait_ge(mh_ready, b + 1)
                dve.wait_ge(m_whole, b + 1)
                vec.tensor_tensor(ML[:, :, :], m_full, MH[:, :, :].bitcast(F32), ALU.subtract
                                  ).then_inc(ml_ready, 1)

            small = {AHEAD - 1: [norms_q, finish_tqT, norms_k], 7: [make_logits], 8: [normalise, attn_bias],
                     12: [out_bias, map_whole, map_low]}

            def step(b, par, following, after):
                for u in range(AHEAD - 1, UNITS):
                    if following and u >= AHEAD:
                        unit_low(b + 1, u)
                    for f in small.get(u, []):
                        f(b)
                dve.wait_ge(c_ready, CB * b + CB)
                for t in range(TILES):
                    dve.wait_ge(o_ready, b * (CB * TILES) + t * CB + 2)
                    out_free(dve, b, t)
                    vec.tensor_scalar(OT[t % OUTS][:, 1, :], obank[(t * CB + 1) % OBANKS][:, 0:TN],
                                      c_out[:, 1:2], None, ALU.add).then_inc(o_taken[1], 1)
                    if following and t == TOP_AT:
                        gram_top(b + 1)
                    if following and t == WHOLE_AT:
                        gram_whole(b + 1)
                    if following and t == LOW_AT:
                        gram_low(b + 1)
                    if after:
                        for u in range(t * FULL // (TILES - 1), min((t + 1) * FULL // (TILES - 1), FULL)):
                            turn(b + 2, u)
                    if following and t == TILES - 1:
                        sums(b + 1)
                    if after and t >= TILES - AHEAD:
                        unit_low(b + 2, t - (TILES - AHEAD))

            for u in range(FULL):
                turn(0, u)
            for u in range(UNITS):
                unit_low(0, u)
            gram_top(0)
            gram_whole(0)
            gram_low(0)
            sums(0)
            for u in range(FULL):
                turn(1, u)
            for u in range(AHEAD):
                unit_low(1, u)
            each_batch(dve, step)

        @block.tensor
        def _(pe):
            ten = nc.tensor

            def transpose_last(b, par):
                pe.wait_ge(loaded[par][TILES - 1], uses(b, par))
                if not isinstance(b, int) or b > 0:
                    pe.wait_ge(xT_low, b * UNITS)
                for k in range(CB):
                    last = ten.transpose(lbank[:, k * P:(k + 1) * P], X[par][:, k, N - P:N], ident[:, :])
                last.then_inc(last_ready, 1)

            def gram_unit(b, u):
                pe.wait_ge(xT_low, b * UNITS + u + 1)
                if u == 0 and not (isinstance(b, int) and b == 0):
                    pe.wait_ge(gram_copied, 2 * b)
                for ch in range(unit_chunks(u)):
                    xt = XT[u % RING][chunk_rows(u), ch, :]
                    flags = dict(start=(u == 0 and ch == 0), stop=(u == UNITS - 1))
                    ten.matmul(bankA[:, :], xt[:, 0:P], xt, **flags)
                    last = ten.matmul(bankB[:, 0:3 * P], xt[:, P:2 * P], xt[:, P:], **flags)
                last.then_inc(unit_used, 1)

            def gram_transposes(b):
                pe.wait_ge(top_ready, 2 * b + 2)
                parts = [ga[:, 2 * P:3 * P], gb[:, P:2 * P], g_top[:, P:2 * P], gb[:, 2 * P:3 * P]]
                for n, part in enumerate(parts):
                    last = ten.transpose(sbank[0][:, n * P:(n + 1) * P], part, ident[:, :])
                last.then_inc(gT_ready, 1)

            def projections(b):
                pe.wait_ge(sums_ready, 3 * b + 3)
                pe.wait_ge(gl_ready, b + 1)
                for j in range(QK):
                    rows = slice(j * P, (j + 1) * P)
                    terms = [(w, g, k) for k in range(CB) for w, g in ((wqkT_h, GH), (wqkT_h, GL), (wqkT_l, GH))]
                    for i, (w, g, k) in enumerate(terms):
                        last = ten.matmul(T_BANKS[j][:, 0:GC], w[:, k, rows], g[:, k, :],
                                          start=(i == 0), stop=(i == len(terms) - 1))
                    last.then_inc(t_ready, 1)

            def tq_transposes(b):
                pe.wait_ge(t_copied, CB * b + CB)
                for k in range(CB):
                    for j in range(CB):
                        last = ten.transpose(obank[2][:, k * C + j * P:k * C + (j + 1) * P],
                                             T[:, j, k * P:(k + 1) * P], ident[:, :])
                last.then_inc(tqT_ready, 1)

            def scores(b):
                pe.wait_ge(tqT_copied, CB * b + CB)
                for j in range(CB):
                    for k in range(CB):
                        last = ten.matmul(sbank[1][:, j * P:(j + 1) * P], tqT[:, k, j * P:(j + 1) * P],
                                          wqkT[:, k, C + j * P:C + (j + 1) * P], start=(k == 0), stop=(k == CB - 1))
                pe.wait_ge(r_ready, b + 1)
                for j in range(CB):
                    last = ten.transpose(sbank[0][:, j * P:(j + 1) * P],
                                         r_n[:, CB + j:CB + j + 1].to_broadcast([P, P]), ident[:, :])
                last.then_inc(s_ready, 1)

            def project_attn(b):
                pe.wait_ge(attn_ready, 2 * b + 2)
                for j in range(CB):
                    last = ten.matmul(obank[2][:, j * C:(j + 1) * C], attn[:, j, :], wpT[:, j, :], start=True, stop=True)
                last.then_inc(pa_ready, 1)

            def spread_bias(b):
                pe.wait_ge(av_ready, CB * b + CB)
                for j in range(CB):
                    last = ten.transpose(sbank[0][:, j * P:(j + 1) * P], av[:, j:j + 1].to_broadcast([P, P]),
                                         ident[:, :])
                last.then_inc(av_spread, 1)

            def whole_map(b):
                pe.wait_ge(pa_copied, b + 1)
                for k in range(CB):
                    for j in range(CB):
                        last = ten.matmul(obank[0][:, k * C:(k + 1) * C], w_nat[:, QK + j, k * P:(k + 1) * P],
                                          pa[:, j, :], start=(j == 0), stop=(j == CB - 1))
                last.then_inc(m_ready, 1)

            def output(b, following):
                pe.wait_ge(ml_ready, b + 1)
                pe.wait_ge(x_low, (b + 1) * (CB * len(SPLITS)))
                for t in range(TILES):
                    n = slice(t * TN, (t + 1) * TN)
                    for o in range(CB):
                        at = t * CB + o
                        if at >= OBANKS:
                            before = at - OBANKS
                            pe.wait_ge(o_taken[before % CB], b * TILES + before // CB + 1)
                        cols = slice(o * P, (o + 1) * P)
                        terms = [(m, v, k) for k in range(CB) for m, v in ((MH, XH), (MH, XL), (ML, XH))]
                        for i, (m, v, k) in enumerate(terms):
                            last = ten.matmul(obank[at % OBANKS][:, 0:TN], m[:, k, cols], v[:, k, n],
                                              start=(i == 0), stop=(i == len(terms) - 1))
                        last.then_inc(o_ready, 1)
                    if following and t == TRANSPOSES_AT:
                        gram_transposes(b + 1)

            small = {3: [scores], 8: [project_attn], 9: [spread_bias, whole_map]}

            def step(b, par, following, after):
                if following:
                    transpose_last(b + 1, 1 - par)
                    for u in range(FIRST):
                        gram_unit(b + 1, u)
                projections(b)
                tq_transposes(b)
                for u in range(FIRST, UNITS):
                    if following:
                        gram_unit(b + 1, u)
                    for f in small.get(u, []):
                        f(b)
                output(b, following)

            pe.wait_ge(w_ready, WB)
            pe.wait_ge(ident_made, 1)
            for k in range(CB):
                for j in range(QK):
                    last = ten.transpose(obank[k][:, j * P:(j + 1) * P], w_nat[:, j, k * P:(k + 1) * P], ident[:, :])
                last.then_inc(wT_ready, 1)
            for j in range(CB):
                for o in range(CB):
                    last = ten.transpose(obank[2][:, j * C + o * P:j * C + (o + 1) * P],
                                         w_nat[:, 3 * CB + o, j * P:(j + 1) * P], ident[:, :])
            last.then_inc(wT_ready, 1)
            pe.wait_ge(wT_copied, 2 * CB + 1)
            transpose_last(0, 0)
            for u in range(UNITS):
                gram_unit(0, u)
            gram_transposes(0)
            each_batch(pe, step)


def kernel(**inputs):
    import numpy as np
    import concourse.bacc as bacc
    from concourse.bass_utils import run_bass_kernel_spmd

    nc = bacc.Bacc("TRN2", target_bir_lowering=False, num_devices=1,
                   dynamic_dma_scratch_size=1024)
    names = ["x", "L0_conv_qkv_w", "L0_conv_qkv_b", "L0_conv_qkv_gain", "L0_conv_proj_w", "L0_conv_proj_b",
             "L0_conv_proj_gain", "L0_conv_temperature"]
    shape = inputs["x"].shape
    arrays, args = {}, []
    for name in names:
        a = np.ascontiguousarray(inputs[name])
        if name == "x":
            a = a.reshape(shape[0], shape[1], shape[2] * shape[3])
        arrays[f"in_{name}"] = a
        args.append(nc.dram_tensor(f"in_{name}", a.shape, mybir.dt.from_np(a.dtype), kind="ExternalInput").ap())
    out = nc.dram_tensor("out", arrays["in_x"].shape, mybir.dt.float32, kind="ExternalOutput").ap()
    channel_attention(nc, *args, out)
    r = run_bass_kernel_spmd(nc, [arrays], core_ids=[0])
    return r.results[0]["out"].reshape(shape)
```

```python
import concourse.bass as bass
from concourse import mybir
from concourse.alu_op_type import AluOpType as ALU
from contextlib import ExitStack



def channel_attention(nc, x, qkv_w, qkv_b, qkv_gain, proj_w, proj_b, proj_gain, temperature, out):
    F32, F32R = mybir.dt.float32, mybir.dt.float32r
    ACT, AX = mybir.ActivationFunctionType, mybir.AxisListType

    P = 128
    BATCH, C, N = x.shape
    HEADS = temperature.shape[0]
    DH = C // HEADS
    CB = C // P
    HPB = P // DH
    QK = 2 * CB
    WB = 4 * CB
    EPS_STD, EPS_L2 = 1e-6, 1e-12
    MASKED = 1e30
    HIGHEST = 3e38
    assert CB == 2 and BATCH % 2 == 0 and BATCH >= 6 and P // DH == 4

    Q = 32
    NQ = P // Q
    UNIT = 2 * P
    FULL = N // UNIT
    R = FULL * UNIT // NQ
    LAST = N - FULL * UNIT
    UNITS = FULL + 1
    assert 0 < LAST <= P
    RING = 4
    FIRST_BANKS = 4
    EARLY_UNITS = 2
    LEAD = 3
    AHEAD = 4
    TILES = 7
    TN = N // TILES
    SPLITS = [(0, 2), (2, 4), (4, 6), (6, 7)]
    LAST_SPLIT = len(SPLITS) - 1
    OUTS = 3
    OBANKS = 3
    assert SPLITS[-1] == (TILES - 1, TILES) and TN * TILES == N and TN % 2 == 0 and TN <= 512
    GC = C + 2

    ctx = ExitStack()
    with ctx:
        def sb(name, shape, dt=F32):
            return ctx.enter_context(nc.sbuf_tensor(name, shape, dt))

        def bank(name):
            return ctx.enter_context(nc.psum_tensor(name, [P, 512], F32))

        def sem(name):
            return ctx.enter_context(nc.semaphore(name))

        X = [sb(f"x{k}", [P, CB, N]) for k in range(2)]
        XH = sb("x_high", [P, CB, N], F32R)
        XL = sb("x_low", [P, CB, N], F32R)
        OT = [sb(f"out_tile{k}", [P, CB, TN]) for k in range(OUTS)]
        Y = sb("x_quads", [P, C // Q, R])
        YT = sb("x_turned", [P, FULL, 2 * C])
        XT = [sb(f"xT{r}", [P, 2, 2 * C], F32R) for r in range(RING)]

        ident = sb("ident", [P, P])
        mask = sb("mask", [P, P])
        w_nat = sb("w_nat", [P, WB - CB, C + 1])
        v_nat = OT[1][:, :, 0:C]
        w_gain = sb("w_gain", [P, WB])
        w_mean = sb("w_mean", [P, WB])
        w_var = sb("w_var", [P, WB])
        w_rstd = sb("w_rstd", [P, WB])
        w_scale = sb("w_scale", [P, WB])
        bias = sb("bias", [P, WB])
        wkT = sb("wkT", [P, CB, C])
        wqkT_h = sb("wqkT_high", [P, CB, QK * P], F32R)
        wqkT_l = sb("wqkT_low", [P, CB, QK * P], F32R)
        wv_h = sb("wv_high", [P, CB, C], F32R)
        wv_l = sb("wv_low", [P, CB, C], F32R)
        wpT = sb("wpT", [P, CB, C])
        nb = sb("nb", [P, QK])
        nbb = sb("nbb", [P, QK])
        bq_row = sb("bq_row", [P, C])
        bk_row = sb("bk_row", [P, C])
        bv_row = sb("bv_row", [P, C])
        eye = sb("eye", [P, CB, C], F32R)
        temp = sb("temp", [P, CB])
        neg_temp = sb("neg_temp", [P, CB])
        half = sb("half", [P, WB])

        s_part = sb("s_part", [P, CB, len(SPLITS)])
        ga = sb("ga", [P, 4 * P])
        junk = ga
        gb = sb("gb", [P, 3 * P])
        g_top = sb("g_top", [P, 2 * P])
        g_low = sb("g_low", [P, P])
        G = sb("G", [P, CB, GC])
        GH = sb("G_high", [P, CB, GC], F32R)
        GL = sb("G_low", [P, CB, GC], F32R)
        T = sb("T", [P, CB, GC])
        n_sq = sb("n_sq", [P, QK])
        n_cl = sb("n_cl", [P, QK])
        r_n = sb("r_n", [P, QK])
        q_scale = sb("q_scale", [P, CB])
        waited = sb("waited", [P, 1])
        q_sum = sb("q_sum", [P, CB])
        tqT = sb("tqT", [P, CB, C])
        logits = sb("logits", [P, CB, P])
        neg_max = sb("neg_max", [P, CB])
        e_sum = sb("e_sum", [P, CB])
        r_sum = sb("r_sum", [P, CB])
        attn = sb("attn", [P, CB, P])
        pa_h = GH[:, :, 0:C]
        pa_l = GL[:, :, 0:C]
        av = sb("av", [P, CB])
        MH = sb("m_high", [P, CB, C], F32R)
        ML = sb("m_low", [P, CB, C], F32R)
        c_out = sb("c_out", [P, CB])

        bankA, bankB = bank("gram_bank0"), bank("gram_bank1")
        lbank = bank("last_unit_bank")
        sbank = [bank("small_bank0"), bank("small_bank1")]
        obank = [bank(f"out_bank{k}") for k in range(OBANKS)]

        weights_in = sem("weights_in")
        columns_in = sem("columns_in")
        temps_in = sem("temps_in")
        rows_in = sem("rows_in")
        ident_made = sem("ident_made")
        pool_made = sem("pool_made")
        var_ready = sem("var_ready")
        rstd_ready = sem("rstd_ready")
        prep_dve = sem("prep_dve")
        squares_ready = sem("squares_ready")
        w_ready = sem("w_ready")
        wT_ready = sem("wT_ready")
        wT_copied = sem("wT_copied")
        wT_low = sem("wT_low")
        loaded = [[sem(f"loaded{k}_{t}") for t in range(TILES)] for k in range(2)]
        quads_in = [sem(f"quads_in{i}") for i in range(NQ)]
        stored = [sem(f"stored{k}") for k in range(OUTS)]
        quads_used = sem("quads_used")
        first_ready = sem("first_ready")
        last_ready = sem("last_ready")
        xT_high = sem("xT_high")
        xT_low = sem("xT_low")
        unit_used = sem("unit_used")
        gram_copied = sem("gram_copied")
        top_ready = sem("top_ready")
        gT_ready = sem("gT_ready")
        g_ready = sem("g_ready")
        sums_ready = sem("sums_ready")
        gh_ready = sem("gh_ready")
        gl_ready = sem("gl_ready")
        t_ready = sem("t_ready")
        t_copied = sem("t_copied")
        tqT_ready = sem("tqT_ready")
        tqT_copied = sem("tqT_copied")
        n_ready = sem("n_ready")
        r_ready = sem("r_ready")
        s_ready = sem("s_ready")
        logits_ready = sem("logits_ready")
        exp_done = sem("exp_done")
        attn_ready = sem("attn_ready")
        av_ready = sem("av_ready")
        av_spread = sem("av_spread")
        c_ready = sem("c_ready")
        pa_ready = sem("pa_ready")
        pa_copied = sem("pa_copied")
        pal_ready = sem("pal_ready")
        m_ready = sem("m_ready")
        mh_ready = sem("mh_ready")
        ml_ready = sem("ml_ready")
        qsum_ready = sem("qsum_ready")
        last_summed = sem("last_summed")
        dve_chain = sem("dve_chain")
        x_high = sem("x_high")
        x_low = sem("x_low")
        o_ready = sem("o_ready")
        o_taken = [sem(f"o_taken{k}") for k in range(CB)]

        def weight_rows(t):
            if QK <= t < QK + CB:
                return v_nat[:, t - QK, :]
            return w_nat[:, t if t < QK else t - CB, 0:C]

        def chunk_rows(u):
            return slice(P - LAST, P) if u == FULL else slice(0, P)

        def unit_chunks(u):
            return 1 if u == FULL else 2

        def unit_source(b, u):
            if u == FULL:
                whole = lbank[chunk_rows(u), 0:C]
            else:
                whole = first_bank(u)[:, :] if isinstance(b, int) and b == 0 else YT[:, u, :]
            return whole.rearrange("p (k c) -> p k c", c=C)

        def first_bank(u):
            banks = [sbank[0], sbank[1], obank[0], obank[1]]
            return lbank if u == FULL else banks[u % len(banks)]

        def tiles_for(pixels):
            return (pixels + TN - 1) // TN

        def uses(b, par):
            return 16 * (b // 2 + 1) if isinstance(b, int) else (b - par) * 8 + 16

        def out_uses(t):
            return len(range(t % OUTS, TILES, OUTS)), t // OUTS

        def each_batch(engine, step):
            step(0, 0, True, True)
            with engine.Fori(1, BATCH - 3, 2) as i:
                step(i, 1, True, True)
                step(i + 1, 0, True, True)
            step(BATCH - 3, 1, True, True)
            step(BATCH - 2, 0, True, False)
            step(BATCH - 1, 1, False, False)

        TOP_AT, TRANSPOSES_AT, WHOLE_AT, HIGH_AT, LOW_AT, SUMS_AT = 1, 2, 3, 4, 5, 5
        T_BANKS = [sbank[0], sbank[1], obank[0], obank[1]]

        def out_free(engine, b, t):
            count, place = out_uses(t)
            if not isinstance(b, int) or b > 0 or place > 0:
                engine.wait_ge(stored[t % OUTS], (b * count + place) * 16)

        block = ctx.enter_context(nc.Block())

        @block.sync
        def _(sp):
            def load(b, par, t):
                sp.dma_start(X[par][:, :, t * TN:(t + 1) * TN],
                             x[b, :, t * TN:(t + 1) * TN].rearrange("(k p) n -> p k n", p=P)
                             ).then_inc(loaded[par][t], 16)

            def gather(b, par, quads=range(NQ)):
                for i in quads:
                    for t in range(tiles_for(i * R), tiles_for((i + 1) * R)):
                        sp.wait_ge(loaded[par][t], uses(b, par))
                    for q in range(NQ):
                        sp.dma_start(Y[i * Q:(i + 1) * Q, q:C // Q:NQ, :],
                                     X[par][q * Q:(q + 1) * Q, :, i * R:(i + 1) * R]).then_inc(quads_in[i], 16)

            def step(b, par, following, after):
                if after:
                    for m, tiles in enumerate(SPLITS):
                        if m == LAST_SPLIT:
                            sp.wait_ge(quads_used, (b + 1) * FULL)
                            gather(b + 2, par, range(NQ // 2))
                        sp.wait_ge(x_low, b * (CB * len(SPLITS)) + CB * (m + 1))
                        if m == 0 and isinstance(b, int) and b == 0:
                            sp.wait_ge(last_summed, 1)
                            sp.wait_ge(last_ready, 1)
                        for t in range(*tiles):
                            load(b + 2, par, t)
                    gather(b + 2, par, range(NQ // 2, NQ))

            for t in range(TILES):
                if t == 2:
                    sp.dma_start(w_nat[:, 0:QK, 0:C], qkv_w[0:2 * C, :].rearrange("(t p) c -> p t c", p=P)
                                 ).then_inc(weights_in, 16)
                    sp.dma_start(v_nat, qkv_w[2 * C:3 * C, :].rearrange("(t p) c -> p t c", p=P)
                                 ).then_inc(weights_in, 16)
                    sp.dma_start(w_nat[:, QK:QK + CB, 0:C], proj_w.rearrange("(t p) c -> p t c", p=P)
                                 ).then_inc(weights_in, 16)
                load(0, 0, t)
            with nc.allow_non_contiguous_dma(reason="columns of biases and gains, once"):
                sp.dma_start(w_gain[:, 0:3 * CB], qkv_gain.rearrange("(t p) -> p t", p=P)).then_inc(columns_in, 16)
                sp.dma_start(w_gain[:, 3 * CB:WB], proj_gain.rearrange("(t p) -> p t", p=P)).then_inc(columns_in, 16)
                sp.dma_start(bias[:, 0:3 * CB], qkv_b.rearrange("(t p) -> p t", p=P)).then_inc(columns_in, 16)
                sp.dma_start(bias[:, 3 * CB:WB], proj_b.rearrange("(t p) -> p t", p=P)).then_inc(columns_in, 16)
            for t in range(TILES):
                load(1, 1, t)
            gather(1, 1)
            for h in range(HEADS):
                j, q = h // HPB, h % HPB
                sp.dma_start(temp[q * DH:(q + 1) * DH, j:j + 1],
                             temperature[h, :, :].to_broadcast([DH, 1])).then_inc(temps_in, 16)
            for row, n0 in ((bq_row, 0), (bk_row, C), (bv_row, 2 * C)):
                sp.dma_start(row[:, :], qkv_b[n0:n0 + C].rearrange("(a n) -> a n", a=1).to_broadcast([P, C])
                             ).then_inc(rows_in, 16)
            each_batch(sp, step)
            for k in range(OUTS):
                sp.wait_ge(stored[k], 16 * BATCH * out_uses(k)[0])

        @block.gpsimd
        def _(pool):
            nc.gpsimd.memset(ident[:, :], 0.0).then_inc(pool_made, 1)
            nc.gpsimd.memset(half[:, :], -0.5).then_inc(pool_made, 1)
            nc.gpsimd.memset(G[:, :, C:GC], 0.0).then_inc(pool_made, 1)
            pool.wait_ge(pool_made, 3)
            nc.gpsimd.affine_select(out=ident[:, :], in_=ident[:, :], compare_op=ALU.not_equal, fill=1.0,
                                    base=0, pattern=[[-1, P]], channel_multiplier=1).then_inc(ident_made, 1)

            def split_low(b, par, m):
                n = slice(SPLITS[m][0] * TN, SPLITS[m][1] * TN)
                for k in range(CB):
                    pool.wait_ge(x_high, b * (CB * len(SPLITS)) + CB * m + k + 1)
                    nc.gpsimd.tensor_tensor(XL[:, k, n], X[par][:, k, n], XH[:, k, n].bitcast(F32), ALU.subtract
                                            ).then_inc(x_low, 1)

            def step(b, par, following, after):
                pool.wait_ge(n_ready, b + 1)
                nc.gpsimd.tensor_tensor(r_n[:, :], n_cl[:, :], half[:, 0:QK], ALU.pow).then_inc(r_ready, 1)
                if following:
                    for m in range(len(SPLITS)):
                        split_low(b + 1, 1 - par, m)

            for m in range(len(SPLITS)):
                if m == 2:
                    pool.wait_ge(ident_made, 1)
                    pool.wait_ge(var_ready, 1)
                    nc.gpsimd.tensor_tensor(w_rstd[:, :], w_var[:, :], half[:, :], ALU.pow).then_inc(rstd_ready, 1)
                split_low(0, 0, m)
            each_batch(pool, step)

        @block.scalar
        def _(act):
            def split_high(b, par, m):
                for t in range(*SPLITS[m]):
                    act.wait_ge(loaded[par][t], uses(b, par))
                n = slice(SPLITS[m][0] * TN, SPLITS[m][1] * TN)
                for k in range(CB):
                    total = dict(accum_out=s_part[:, k, m:m + 1]) if m < LAST_SPLIT else {}
                    nc.scalar.activation(XH[:, k, n], X[par][:, k, n], ACT.Copy, **total).then_inc(x_high, 1)

            def unit_high(b, u):
                if u == FULL:
                    act.wait_ge(last_ready, b + 1)
                elif isinstance(b, int) and b == 0:
                    act.wait_ge(first_ready, u + 1)
                else:
                    act.wait_ge(quads_used, (b - 1) * FULL + u + 1)
                if u >= RING:
                    act.wait_ge(unit_used, b * UNITS + u - RING + 1)
                nc.scalar.activation(XT[u % RING][chunk_rows(u), 0:unit_chunks(u), 0:C], unit_source(b, u), ACT.Copy
                                     ).then_inc(xT_high, 1)

            def store(b, t):
                for k in range(CB):
                    act.wait_ge(o_taken[k], b * TILES + t + 1)
                act.dma_start(out[b, :, t * TN:(t + 1) * TN].rearrange("(k p) n -> p k n", p=P),
                              OT[t % OUTS][:, :, :]).then_inc(stored[t % OUTS], 16)

            def copy_gram(b):
                act.wait_ge(unit_used, (b + 1) * UNITS)
                nc.scalar.activation(ga[:, :], bankA[:, :], ACT.Copy).then_inc(gram_copied, 1)
                nc.scalar.activation(gb[:, :], bankB[:, 0:3 * P], ACT.Copy).then_inc(gram_copied, 1)

            def gram_high(b):
                act.wait_ge(g_ready, 3 * b + 3)
                nc.scalar.activation(GH[:, :, 0:C], G[:, :, 0:C], ACT.Copy).then_inc(gh_ready, 1)

            def copy_t(b):
                for j in range(CB):
                    act.wait_ge(t_ready, b * QK + j + 1)
                    nc.scalar.activation(T[:, j, :], T_BANKS[j][:, 0:GC], ACT.Copy).then_inc(t_copied, 1)

            def exps(b):
                for j in range(CB):
                    act.wait_ge(logits_ready, b * CB + j + 1)
                    nc.scalar.activation(attn[:, j, :], logits[:, j, :], ACT.Exp, scale=-1.0,
                                         bias=neg_max[:, j:j + 1], accum_out=e_sum[:, j:j + 1]).then_inc(exp_done, 1)

            def copy_pa(b):
                act.wait_ge(pa_ready, b + 1)
                nc.scalar.activation(pa_h, obank[2][:, :].rearrange("p (k c) -> p k c", c=C), ACT.Copy
                                     ).then_inc(pa_copied, 1)

            def map_high(b):
                for k in range(CB):
                    act.wait_ge(m_ready, b * CB + k + 1)
                    nc.scalar.activation(MH[:, k, :], obank[k][:, 0:C], ACT.Copy).then_inc(mh_ready, 1)

            small = {3: [copy_t], 8: [exps], 12: [copy_pa, map_high]}

            def step(b, par, following, after):
                for u in range(AHEAD - 1, UNITS):
                    if following and u >= AHEAD:
                        unit_high(b + 1, u)
                    for f in small.get(u, []):
                        f(b)
                act.wait_ge(c_ready, CB * b + CB)
                if following:
                    copy_gram(b + 1)
                for t in range(TILES):
                    act.wait_ge(o_ready, b * (CB * TILES) + t * CB + 1)
                    out_free(act, b, t)
                    nc.scalar.activation(OT[t % OUTS][:, 0, :], obank[t * CB % OBANKS][:, 0:TN], ACT.Identity,
                                         bias=c_out[:, 0:1]).then_inc(o_taken[0], 1)
                    if t > 0:
                        store(b, t - 1)
                    for m, (_, end) in enumerate(SPLITS):
                        if following and end == t + 1:
                            act.wait_ge(o_ready, b * (CB * TILES) + CB * end)
                            split_high(b + 1, 1 - par, m)
                    if following and t == HIGH_AT:
                        gram_high(b + 1)
                    if after and t >= TILES - AHEAD:
                        unit_high(b + 2, t - (TILES - AHEAD))
                store(b, TILES - 1)

            for u in range(UNITS):
                unit_high(0, u)
                if u % 4 == 3:
                    split_high(0, 0, u // 4)
            copy_gram(0)
            split_high(0, 0, LAST_SPLIT)
            for k in range(3):
                act.wait_ge(wT_ready, k + 1)
                if k < CB:
                    nc.scalar.activation(wqkT_h[:, k, :], obank[k][:, :], ACT.Copy).then_inc(wT_copied, 1)
                    nc.scalar.activation(wkT[:, k, :], obank[k][:, C:2 * C], ACT.Copy).then_inc(wT_copied, 1)
                else:
                    nc.scalar.activation(wpT[:, :, :], obank[2][:, :].rearrange("p (k c) -> p k c", c=C), ACT.Copy
                                         ).then_inc(wT_copied, 1)
            nc.scalar.activation(wv_h[:, :, :], v_nat, ACT.Copy).then_inc(wT_copied, 1)
            gram_high(0)
            for u in range(AHEAD):
                unit_high(1, u)
            each_batch(act, step)

        @block.vector
        def _(dve):
            vec = nc.vector
            done = [0]

            def prep(instruction):
                instruction.then_inc(prep_dve, 1)
                done[0] += 1
                dve.wait_ge(prep_dve, done[0])

            prep(vec.memset(mask[:, :], MASKED))
            for q in range(HPB):
                prep(vec.memset(mask[q * DH:(q + 1) * DH, q * DH:(q + 1) * DH], 0.0))
            dve.wait_ge(ident_made, 1)
            for k in range(CB):
                for j in range(CB):
                    prep(vec.tensor_scalar(eye[:, k, j * P:(j + 1) * P], ident[:, :], float(j == k), None, ALU.mult))

            def turn(b, u):
                if u == 0:
                    for i in range(NQ):
                        dve.wait_ge(quads_in[i], b * (16 * NQ))
                if not isinstance(b, int) or b > 1:
                    dve.wait_ge(xT_low, b * UNITS - UNITS + u + 1)
                vec.transpose(YT[:, u, :].rearrange("p (j g a) -> p j g a", j=2, a=Q),
                              Y[:, :, u * 2 * Q:(u + 1) * 2 * Q].rearrange("p g (j a) -> p j g a", a=Q)
                              ).then_inc(quads_used, 1)

            def unit_low(b, u):
                tile = XT[u % RING][chunk_rows(u), 0:unit_chunks(u), :]
                dve.wait_ge(xT_high, b * UNITS + u + 1)
                vec.tensor_tensor(tile[:, :, C:2 * C], unit_source(b, u), tile[:, :, 0:C].bitcast(F32), ALU.subtract
                                  ).then_inc(xT_low, 1)

            def gram_top(b):
                dve.wait_ge(gram_copied, 2 * b + 2)
                vec.tensor_tensor(g_top[:, :], ga[:, 0:2 * P], ga[:, 2 * P:4 * P], ALU.add).then_inc(top_ready, 1)
                vec.tensor_tensor(g_low[:, :], gb[:, 0:P], gb[:, 2 * P:3 * P], ALU.add).then_inc(top_ready, 1)

            def gram_whole(b):
                dve.wait_ge(gT_ready, b + 1)
                dve.wait_ge(top_ready, 2 * b + 2)
                vec.tensor_tensor(G[:, 0, 0:C], g_top[:, :], sbank[0][:, 0:2 * P], ALU.add).then_inc(g_ready, 1)
                vec.tensor_tensor(G[:, 1, 0:P], gb[:, P:2 * P], sbank[0][:, 2 * P:3 * P], ALU.add
                                  ).then_inc(g_ready, 1)
                vec.tensor_tensor(G[:, 1, P:C], g_low[:, :], sbank[0][:, 3 * P:4 * P], ALU.add).then_inc(g_ready, 1)

            def gram_low(b):
                dve.wait_ge(gh_ready, b + 1)
                dve.wait_ge(g_ready, 3 * b + 3)
                vec.tensor_tensor(GL[:, :, 0:C], G[:, :, 0:C], GH[:, :, 0:C].bitcast(F32), ALU.subtract
                                  ).then_inc(gl_ready, 1)

            def sum_last(b, par):
                dve.wait_ge(loaded[par][TILES - 1], uses(b, par))
                if not isinstance(b, int) or b > 0:
                    dve.wait_ge(sums_ready, 3 * b)
                vec.reduce_sum(s_part[:, :, LAST_SPLIT:], X[par][:, :, (TILES - 1) * TN:], AX.X
                               ).then_inc(last_summed, 1)

            def sums(b):
                behind = slice(C, GC)
                dve.wait_ge(x_high, b * (CB * len(SPLITS)) + CB * LAST_SPLIT)
                dve.wait_ge(last_summed, b + 1)
                vec.reduce_sum(G[:, :, C:C + 1], s_part[:, :, :], AX.X).then_inc(sums_ready, 1)
                dve.wait_ge(sums_ready, 3 * b + 1)
                vec.tensor_copy(GH[:, :, behind], G[:, :, behind]).then_inc(sums_ready, 1)
                dve.wait_ge(sums_ready, 3 * b + 2)
                vec.tensor_tensor(GL[:, :, behind], G[:, :, behind], GH[:, :, behind].bitcast(F32), ALU.subtract
                                  ).then_inc(sums_ready, 1)

            CHAIN = 10

            def norms(b, blocks):
                for j in blocks:
                    if j < CB:
                        dve.wait_ge(t_copied, b * CB + j + 1)
                        t_j = T[:, j, :]
                    else:
                        dve.wait_ge(t_ready, b * QK + j + 1)
                        t_j = T_BANKS[j]
                    if j > 0:
                        dve.wait_ge(dve_chain, b * CHAIN + j)
                    vec.tensor_tensor_reduce(out=junk[:, 0:C + 1], in0=t_j[:, 0:C + 1], in1=w_nat[:, j, :], scale=1.0,
                                             scalar=nbb[:, j:j + 1], op0=ALU.mult, op1=ALU.add,
                                             accum_out=n_sq[:, j:j + 1]).then_inc(dve_chain, 1)

            def norms_q(b):
                norms(b, range(CB))
                vec.tensor_tensor(q_sum[:, :], T[:, 0:CB, C], nb[:, 0:CB], ALU.add).then_inc(qsum_ready, 1)

            def norms_k(b):
                norms(b, range(CB, QK))
                dve.wait_ge(dve_chain, b * CHAIN + 4)
                vec.tensor_scalar(n_cl[:, :], n_sq[:, :], EPS_L2 * EPS_L2, None, ALU.max).then_inc(n_ready, 1)

            def finish_tqT(b):
                dve.wait_ge(tqT_ready, b + 1)
                for k in range(CB):
                    vec.scalar_tensor_tensor(tqT[:, k, :], bq_row[:, :], G[:, k, C:C + 1],
                                             obank[2][:, k * C:(k + 1) * C], ALU.mult, ALU.add
                                             ).then_inc(tqT_copied, 1)

            def make_logits(b):
                dve.wait_ge(r_ready, b + 1)
                vec.tensor_tensor(q_scale[:, :], r_n[:, 0:CB], neg_temp[:, :], ALU.mult).then_inc(dve_chain, 1)
                dve.wait_ge(s_ready, b + 1)
                dve.wait_ge(qsum_ready, b + 1)
                for j in range(CB):
                    vec.scalar_tensor_tensor(logits[:, j, :], bk_row[:, j * P:(j + 1) * P], q_sum[:, j:j + 1],
                                             sbank[1][:, j * P:(j + 1) * P], ALU.mult, ALU.add
                                             ).then_inc(dve_chain, 1)
                for j in range(CB):
                    dve.wait_ge(dve_chain, b * CHAIN + 6 + j)
                    vec.scalar_tensor_tensor(logits[:, j, :], logits[:, j, :], q_scale[:, j:j + 1],
                                             sbank[0][:, j * P:(j + 1) * P], ALU.mult, ALU.mult
                                             ).then_inc(dve_chain, 1)
                dve.wait_ge(dve_chain, b * CHAIN + 9)
                vec.tensor_copy(waited[:, :], q_scale[:, 0:1])
                for j in range(CB):
                    vec.tensor_tensor_reduce(out=logits[:, j, :], in0=mask[:, :], in1=logits[:, j, :],
                                             scale=1.0, scalar=HIGHEST, op0=ALU.add, op1=ALU.min,
                                             accum_out=neg_max[:, j:j + 1]).then_inc(logits_ready, 1)

            def normalise(b):
                dve.wait_ge(exp_done, 2 * b + 2)
                vec.reciprocal(r_sum[:, :], e_sum[:, :]).then_inc(dve_chain, 1)
                dve.wait_ge(dve_chain, b * CHAIN + 10)
                for j in range(CB):
                    vec.tensor_scalar(attn[:, j, :], attn[:, j, :], r_sum[:, j:j + 1], None, ALU.mult
                                      ).then_inc(attn_ready, 1)

            def pa_low(b):
                dve.wait_ge(pa_copied, b + 1)
                vec.tensor_tensor(pa_l, obank[2][:, :].rearrange("p (k c) -> p k c", c=C), pa_h.bitcast(F32),
                                  ALU.subtract).then_inc(pal_ready, 1)

            def attn_bias(b):
                dve.wait_ge(attn_ready, CB * b + CB)
                for j in range(CB):
                    vec.tensor_tensor_reduce(out=junk[:, j * P:(j + 1) * P], in0=attn[:, j, :],
                                             in1=bv_row[:, j * P:(j + 1) * P], scale=1.0, scalar=0.0,
                                             op0=ALU.mult, op1=ALU.add, accum_out=av[:, j:j + 1]
                                             ).then_inc(av_ready, 1)

            def out_bias(b):
                dve.wait_ge(av_spread, b + 1)
                for o in range(CB):
                    vec.tensor_tensor_reduce(out=junk[:, o * C:(o + 1) * C], in0=sbank[0][:, 0:C],
                                             in1=w_nat[:, QK + o, 0:C], scale=1.0,
                                             scalar=bias[:, 3 * CB + o:3 * CB + o + 1],
                                             op0=ALU.mult, op1=ALU.add, accum_out=c_out[:, o:o + 1]
                                             ).then_inc(c_ready, 1)

            def map_low(b):
                for k in range(CB):
                    dve.wait_ge(mh_ready, b * CB + k + 1)
                    vec.tensor_tensor(ML[:, k, :], obank[k][:, 0:C], MH[:, k, :].bitcast(F32), ALU.subtract
                                      ).then_inc(ml_ready, 1)

            turns = [2, 4, 5, 9, 10, 12, 12, 12]

            small = {3: [norms_q, norms_k, finish_tqT], 7: [make_logits],
                     8: [normalise, attn_bias], 10: [pa_low], 11: [out_bias], 12: [map_low]}

            def step(b, par, following, after):
                for u in range(AHEAD - 1, UNITS):
                    if following and u >= AHEAD:
                        unit_low(b + 1, u)
                    for f in small.get(u, []):
                        f(b)
                dve.wait_ge(c_ready, CB * b + CB)
                if following:
                    sum_last(b + 1, 1 - par)
                if after:
                    for u in range(turns[0]):
                        turn(b + 2, u)
                for t in range(TILES):
                    dve.wait_ge(o_ready, b * (CB * TILES) + t * CB + 2)
                    out_free(dve, b, t)
                    vec.tensor_scalar(OT[t % OUTS][:, 1, :], obank[(t * CB + 1) % OBANKS][:, 0:TN],
                                      c_out[:, 1:2], None, ALU.add).then_inc(o_taken[1], 1)
                    if following and t == TOP_AT:
                        gram_top(b + 1)
                    if following and t == WHOLE_AT:
                        gram_whole(b + 1)
                    if following and t == LOW_AT:
                        gram_low(b + 1)
                    if after:
                        for u in range(turns[t], turns[t + 1]):
                            turn(b + 2, u)
                    if following and t == SUMS_AT:
                        sums(b + 1)
                    if after and t >= TILES - AHEAD:
                        unit_low(b + 2, t - (TILES - AHEAD))

            for u in range(EARLY_UNITS):
                unit_low(0, u)
            dve.wait_ge(weights_in, 16 * 3)
            for t0, rows in ((0, w_nat[:, 0:QK, 0:C]), (QK, v_nat), (QK + CB, w_nat[:, QK:QK + CB, 0:C])):
                prep(vec.reduce_sum(w_mean[:, t0:t0 + rows.shape[1]], rows, AX.X))
            prep(vec.tensor_scalar(w_mean[:, :], w_mean[:, :], 1.0 / C, None, ALU.mult))
            for t in range(WB):
                rows = weight_rows(t)
                prep(vec.tensor_scalar(rows, rows, w_mean[:, t:t + 1], None, ALU.subtract))
                vec.tensor_tensor_reduce(out=OT[0][:, 0, 0:C], in0=rows, in1=rows,
                                         scale=1.0, scalar=0.0, op0=ALU.mult, op1=ALU.add,
                                         accum_out=w_var[:, t:t + 1]).then_inc(squares_ready, 1)
                unit_low(0, EARLY_UNITS + t)
            dve.wait_ge(squares_ready, WB)
            vec.tensor_scalar(w_var[:, :], w_var[:, :], 1.0 / C, EPS_STD, ALU.mult, ALU.add).then_inc(var_ready, 1)
            for u in range(EARLY_UNITS + WB, UNITS):
                unit_low(0, u)
            sum_last(0, 0)
            dve.wait_ge(columns_in, 16 * 4)
            prep(vec.tensor_scalar(w_scale[:, :], w_gain[:, :], float(C) ** -0.5, None, ALU.mult))
            dve.wait_ge(rstd_ready, 1)
            prep(vec.tensor_tensor(w_scale[:, :], w_scale[:, :], w_rstd[:, :], ALU.mult))
            for t in range(WB):
                vec.tensor_scalar(weight_rows(t), weight_rows(t), w_scale[:, t:t + 1], None, ALU.mult
                                  ).then_inc(w_ready, 1)
            gram_top(0)
            dve.wait_ge(w_ready, WB)
            prep(vec.tensor_scalar(w_nat[:, 0:QK, C], bias[:, 0:QK], 2.0, None, ALU.mult))
            prep(vec.tensor_scalar(nb[:, :], bias[:, 0:QK], float(N), None, ALU.mult))
            prep(vec.tensor_tensor(nbb[:, :], nb[:, :], bias[:, 0:QK], ALU.mult))
            gram_whole(0)
            for k in range(CB):
                dve.wait_ge(wT_copied, 2 * k + 2)
                vec.tensor_tensor(wqkT_l[:, k, :], obank[k][:, :], wqkT_h[:, k, :].bitcast(F32), ALU.subtract
                                  ).then_inc(wT_low, 1)
            gram_low(0)
            dve.wait_ge(wT_copied, 2 * CB + 2)
            prep(vec.tensor_tensor(wv_l[:, :, :], v_nat, wv_h[:, :, :].bitcast(F32), ALU.subtract))
            sums(0)
            for u in range(FULL):
                turn(1, u)
            dve.wait_ge(temps_in, 16 * HEADS)
            prep(vec.tensor_scalar(neg_temp[:, :], temp[:, :], -1.0, None, ALU.mult))
            dve.wait_ge(rows_in, 16 * 3)
            for u in range(AHEAD):
                unit_low(1, u)
            each_batch(dve, step)

        @block.tensor
        def _(pe):
            ten = nc.tensor

            def transpose_last(b, par):
                pe.wait_ge(loaded[par][TILES - 1], uses(b, par))
                if not isinstance(b, int) or b > 0:
                    pe.wait_ge(xT_low, b * UNITS)
                for k in range(CB):
                    last = ten.transpose(lbank[:, k * P:(k + 1) * P], X[par][:, k, N - P:N], ident[:, :])
                last.then_inc(last_ready, 1)

            def transpose_first(u):
                for t in range(tiles_for(u * UNIT), tiles_for((u + 1) * UNIT)):
                    pe.wait_ge(loaded[0][t], uses(0, 0))
                if u >= FIRST_BANKS:
                    pe.wait_ge(xT_low, u - FIRST_BANKS + 1)
                for ch in range(2):
                    for k in range(CB):
                        at = (ch * CB + k) * P
                        n = u * UNIT + ch * P
                        last = ten.transpose(first_bank(u)[:, at:at + P], X[0][:, k, n:n + P], ident[:, :])
                last.then_inc(first_ready, 1)

            def gram_unit(b, u):
                pe.wait_ge(xT_low, b * UNITS + u + 1)
                if u == 0 and not (isinstance(b, int) and b == 0):
                    pe.wait_ge(gram_copied, 2 * b)
                for ch in range(unit_chunks(u)):
                    xt = XT[u % RING][chunk_rows(u), ch, :]
                    flags = dict(start=(u == 0 and ch == 0), stop=(u == UNITS - 1))
                    ten.matmul(bankA[:, :], xt[:, 0:P], xt, **flags)
                    last = ten.matmul(bankB[:, 0:3 * P], xt[:, P:2 * P], xt[:, P:], **flags)
                last.then_inc(unit_used, 1)

            def gram_transposes(b):
                pe.wait_ge(top_ready, 2 * b + 2)
                parts = [ga[:, 2 * P:3 * P], gb[:, P:2 * P], g_top[:, P:2 * P], gb[:, 2 * P:3 * P]]
                for n, part in enumerate(parts):
                    last = ten.transpose(sbank[0][:, n * P:(n + 1) * P], part, ident[:, :])
                last.then_inc(gT_ready, 1)

            def projections(b):
                pe.wait_ge(sums_ready, 3 * b + 3)
                pe.wait_ge(gl_ready, b + 1)
                for j in range(QK):
                    if j == CB and not (isinstance(b, int) and b == 0):
                        for k in range(CB):
                            pe.wait_ge(o_taken[k], b * TILES)
                    rows = slice(j * P, (j + 1) * P)
                    terms = [(w, g, k) for k in range(CB) for w, g in ((wqkT_h, GH), (wqkT_h, GL), (wqkT_l, GH))]
                    for i, (w, g, k) in enumerate(terms):
                        last = ten.matmul(T_BANKS[j][:, 0:GC], w[:, k, rows], g[:, k, :],
                                          start=(i == 0), stop=(i == len(terms) - 1))
                    last.then_inc(t_ready, 1)

            def tq_transposes(b):
                pe.wait_ge(t_copied, CB * b + CB)
                for k in range(CB):
                    for j in range(CB):
                        last = ten.transpose(obank[2][:, k * C + j * P:k * C + (j + 1) * P],
                                             T[:, j, k * P:(k + 1) * P], ident[:, :])
                last.then_inc(tqT_ready, 1)

            def scores(b):
                pe.wait_ge(tqT_copied, CB * b + CB)
                for j in range(CB):
                    for k in range(CB):
                        last = ten.matmul(sbank[1][:, j * P:(j + 1) * P], tqT[:, k, j * P:(j + 1) * P],
                                          wkT[:, k, j * P:(j + 1) * P], start=(k == 0), stop=(k == CB - 1))
                pe.wait_ge(r_ready, b + 1)
                for j in range(CB):
                    last = ten.transpose(sbank[0][:, j * P:(j + 1) * P],
                                         r_n[:, CB + j:CB + j + 1].to_broadcast([P, P]), ident[:, :])
                last.then_inc(s_ready, 1)

            def project_attn(b):
                pe.wait_ge(attn_ready, 2 * b + 2)
                for j in range(CB):
                    last = ten.matmul(obank[2][:, j * C:(j + 1) * C], attn[:, j, :], wpT[:, j, :],
                                      start=True, stop=True)
                last.then_inc(pa_ready, 1)

            def spread_bias(b):
                pe.wait_ge(av_ready, CB * b + CB)
                for j in range(CB):
                    last = ten.transpose(sbank[0][:, j * P:(j + 1) * P], av[:, j:j + 1].to_broadcast([P, P]),
                                         ident[:, :])
                last.then_inc(av_spread, 1)

            def whole_map(b):
                pe.wait_ge(pal_ready, b + 1)
                for k in range(CB):
                    part, cols = obank[k][:, 0:C], slice(k * P, (k + 1) * P)
                    ten.matmul(part, eye[:, 0, 0:P], eye[:, k, :], start=True, stop=False)
                    terms = [(w, p, j) for j in range(CB) for w, p in ((wv_h, pa_h), (wv_h, pa_l), (wv_l, pa_h))]
                    for i, (w, p, j) in enumerate(terms):
                        last = ten.matmul(part, w[:, j, cols], p[:, j, :], start=False,
                                          stop=(i == len(terms) - 1))
                    last.then_inc(m_ready, 1)

            def output(b, following):
                pe.wait_ge(x_low, (b + 1) * (CB * len(SPLITS)))
                for t in range(TILES):
                    n = slice(t * TN, (t + 1) * TN)
                    for o in range(CB):
                        at = t * CB + o
                        if at >= OBANKS:
                            before = at - OBANKS
                            pe.wait_ge(o_taken[before % CB], b * TILES + before // CB + 1)
                        cols = slice(o * P, (o + 1) * P)
                        terms = [(m, v, k) for k in range(CB) for m, v in ((MH, XH), (MH, XL), (ML, XH))]
                        for i, (m, v, k) in enumerate(terms):
                            if at == 0 and i % 3 == 0:
                                pe.wait_ge(ml_ready, b * CB + k + 1)
                            last = ten.matmul(obank[at % OBANKS][:, 0:TN], m[:, k, cols], v[:, k, n],
                                              start=(i == 0), stop=(i == len(terms) - 1))
                        last.then_inc(o_ready, 1)
                    if following and t == TRANSPOSES_AT:
                        gram_transposes(b + 1)

            small = {-1: [projections], 0: [tq_transposes], 3: [scores],
                     8: [project_attn, spread_bias], 10: [whole_map]}

            def step(b, par, following, after):
                if following:
                    transpose_last(b + 1, 1 - par)
                for u in range(-1, UNITS):
                    if following and u >= 0:
                        gram_unit(b + 1, u)
                    for f in small.get(u, []):
                        f(b)
                output(b, following)

            pe.wait_ge(ident_made, 1)
            for u in range(UNITS):
                if u < FULL:
                    transpose_first(u)
                else:
                    transpose_last(0, 0)
                if u >= LEAD:
                    gram_unit(0, u - LEAD)
            for u in range(UNITS - LEAD, UNITS):
                gram_unit(0, u)
            pe.wait_ge(w_ready, WB)
            pe.wait_ge(xT_low, UNITS)
            for k in range(CB):
                for j in range(QK):
                    last = ten.transpose(obank[k][:, j * P:(j + 1) * P], w_nat[:, j, k * P:(k + 1) * P], ident[:, :])
                last.then_inc(wT_ready, 1)
            for j in range(CB):
                for o in range(CB):
                    last = ten.transpose(obank[2][:, j * C + o * P:j * C + (o + 1) * P],
                                         w_nat[:, QK + o, j * P:(j + 1) * P], ident[:, :])
            last.then_inc(wT_ready, 1)
            gram_transposes(0)
            pe.wait_ge(wT_copied, 2 * CB + 1)
            pe.wait_ge(wT_low, CB)
            each_batch(pe, step)


def kernel(**inputs):
    import numpy as np
    import concourse.bacc as bacc
    from concourse.bass_utils import run_bass_kernel_spmd

    nc = bacc.Bacc("TRN2", target_bir_lowering=False, num_devices=1,
                   dynamic_dma_scratch_size=1024)
    names = ["x", "L0_conv_qkv_w", "L0_conv_qkv_b", "L0_conv_qkv_gain", "L0_conv_proj_w", "L0_conv_proj_b",
             "L0_conv_proj_gain", "L0_conv_temperature"]
    shape = inputs["x"].shape
    arrays, args = {}, []
    for name in names:
        a = np.ascontiguousarray(inputs[name])
        if name == "x":
            a = a.reshape(shape[0], shape[1], shape[2] * shape[3])
        arrays[f"in_{name}"] = a
        args.append(nc.dram_tensor(f"in_{name}", a.shape, mybir.dt.from_np(a.dtype), kind="ExternalInput").ap())
    out = nc.dram_tensor("out", arrays["in_x"].shape, mybir.dt.float32, kind="ExternalOutput").ap()
    channel_attention(nc, *args, out)
    r = run_bass_kernel_spmd(nc, [arrays], core_ids=[0])
    return r.results[0]["out"].reshape(shape)
```
